# Optimizing a Trainium2 kernel written in Bass

```python
import numpy as np
import jax
import jax.numpy as jnp

def _softmax(x, axis=-1):
    return jax.nn.softmax(x, axis=axis)

def _gelu(x):
    return jax.nn.gelu(x, approximate=True)

def _silu(x):
    return jax.nn.silu(x)

def _sigmoid(x):
    return jax.nn.sigmoid(x)

def _layernorm(x, axis=-1, eps=1e-05):
    m = jnp.mean(x, axis=axis, keepdims=True)
    v = jnp.var(x, axis=axis, keepdims=True)
    return (x - m) / jnp.sqrt(v + eps)

def _scatter_add(tgt, idx, src, axis=0):
    return tgt.at[idx].add(src)

def _segment_sum(src, seg, n):
    return jax.ops.segment_sum(src, seg, n)
kernel_name = 'mk_rec_standalone_d1_rec_r8_fdf15a'

def setup_inputs(seed: int=0):
    np.random.seed(seed)
    _w = jnp.asarray

    def _rec_inputs():
        import jax
        import jax.numpy as jnp
        _rk = jax.random.key(seed)
        r_batch_idxes = jax.random.randint(jax.random.fold_in(_rk, 1), (1024,), 28, 99986, jnp.int32)
        return r_batch_idxes
    r_batch_idxes = _rec_inputs()

    def _L0_rec_setup():
        import jax, jax.numpy as jnp
        import numpy as np
        ITEM_NUMS = 12500
        EMB_DIM = 128
        HID_DIM = 128
        N_ITEMS = 6250
        N_SESS = 6250
        N_TOTAL = N_SESS + N_ITEMS
        NNZ_S = 62500
        NNZ_A = 400000
        BATCH = 256
        N_SCORE = 6250
        key = jax.random.key(seed)
        ks = jax.random.split(key, 12)
        return {'emb_table': jax.random.normal(ks[0], (ITEM_NUMS, EMB_DIM), jnp.float32), 'W': jax.random.normal(ks[1], (EMB_DIM, HID_DIM), jnp.float32) * 0.01, 'b': jax.random.normal(ks[2], (HID_DIM,), jnp.float32) * 0.01, 'sess_vals': jax.random.uniform(ks[3], (NNZ_S,), jnp.float32), 'A_vals': jax.random.uniform(ks[4], (NNZ_A,), jnp.float32), 'batch_idxes': jax.random.randint(ks[5], (BATCH,), 0, N_TOTAL), 'item_idxes': jax.random.randint(ks[6], (N_SCORE,), 0, N_TOTAL), 'item_emb_idxes': jax.random.randint(ks[7], (N_ITEMS,), 0, ITEM_NUMS), 'sess_rows': jax.random.randint(ks[8], (NNZ_S,), 0, N_SESS), 'sess_cols': jax.random.randint(ks[9], (NNZ_S,), 0, N_ITEMS), 'A_rows': jax.random.randint(ks[10], (NNZ_A,), 0, N_TOTAL), 'A_cols': jax.random.randint(ks[11], (NNZ_A,), 0, N_TOTAL)}
    _L0_rec_all = _L0_rec_setup()
    _L0_rec_in = {k: v for k, v in _L0_rec_all.items() if k in ('emb_table', 'W', 'b', 'sess_vals', 'A_vals', 'item_idxes', 'item_emb_idxes', 'sess_rows', 'sess_cols', 'A_rows', 'A_cols')}
    del _L0_rec_all
    return {'r_batch_idxes': r_batch_idxes, 'L0_rec_emb_table': _L0_rec_in['emb_table'], 'L0_rec_W': _L0_rec_in['W'], 'L0_rec_b': _L0_rec_in['b'], 'L0_rec_sess_vals': _L0_rec_in['sess_vals'], 'L0_rec_A_vals': _L0_rec_in['A_vals'], 'L0_rec_item_idxes': _L0_rec_in['item_idxes'], 'L0_rec_item_emb_idxes': _L0_rec_in['item_emb_idxes'], 'L0_rec_sess_rows': _L0_rec_in['sess_rows'], 'L0_rec_sess_cols': _L0_rec_in['sess_cols'], 'L0_rec_A_rows': _L0_rec_in['A_rows'], 'L0_rec_A_cols': _L0_rec_in['A_cols']}

def reference(r_batch_idxes, L0_rec_emb_table, L0_rec_W, L0_rec_b, L0_rec_sess_vals, L0_rec_A_vals, L0_rec_item_idxes, L0_rec_item_emb_idxes, L0_rec_sess_rows, L0_rec_sess_cols, L0_rec_A_rows, L0_rec_A_cols):
    import jax
    import jax.numpy as jnp

    def _L0_rec_ref(emb_table, W, b, sess_vals, A_vals, batch_idxes, item_idxes, item_emb_idxes, sess_rows, sess_cols, A_rows, A_cols):
        import jax, jax.numpy as jnp
        import numpy as np
        ITEM_NUMS = 12500
        EMB_DIM = 128
        HID_DIM = 128
        N_ITEMS = 6250
        N_SESS = 6250
        N_TOTAL = N_SESS + N_ITEMS
        NNZ_S = 62500
        NNZ_A = 400000
        BATCH = 256
        N_SCORE = 6250
        x_item = emb_table[item_emb_idxes]
        x_session = jax.ops.segment_sum(sess_vals[:, None] * x_item[sess_cols], sess_rows, num_segments=N_SESS)
        x = jnp.concatenate((x_session, x_item), axis=0)
        xw = x @ W
        h1 = jax.ops.segment_sum(A_vals[:, None] * xw[A_cols], A_rows, num_segments=N_TOTAL) + b
        out = h1[batch_idxes] @ h1[item_idxes].T
        return out
    y = _L0_rec_ref(L0_rec_emb_table, L0_rec_W, L0_rec_b, L0_rec_sess_vals, L0_rec_A_vals, r_batch_idxes, L0_rec_item_idxes, L0_rec_item_emb_idxes, L0_rec_sess_rows, L0_rec_sess_cols, L0_rec_A_rows, L0_rec_A_cols)
    return y

_drawn_inputs = setup_inputs


def setup_inputs(seed=0):
    import zlib

    import numpy as np

    out = dict(_drawn_inputs(seed))
    spreads = {}
    factors = {}
    for name, (base, spread) in spreads.items():
        noise = np.random.default_rng([zlib.crc32(name.encode()), seed]).standard_normal(out[name].shape)
        drawn = base * np.exp(spread * noise) if base else spread * noise
        out[name] = jnp.asarray(drawn.astype(out[name].dtype))
    for name, factor in factors.items():
        out[name] = (out[name] * factor).astype(out[name].dtype)
    return out
```

```python
from contextlib import ExitStack

import concourse.bass as bass
from concourse import mybir

F32 = mybir.dt.float32
I32 = mybir.dt.int32
BF16 = mybir.dt.bfloat16
ALU = mybir.AluOpType
ACT = mybir.ActivationFunctionType
AX_X = mybir.AxisListType.X

P = 128
D = 128
N_SESS = 6250
N_ITEMS = 6250
N_TOTAL = N_SESS + N_ITEMS
NNZ_S = 62500
NNZ_A = 400000
BATCH = 1024
N_SCORE = 6250

Q = 32
BATCH_Q = 4
NQ = Q // BATCH_Q
U = 8
FLD = 2
OWN = 8192.0
FAR = float(1 << 20)
COL_BITS = 14


class EdgeList:

    def __init__(self, name, nnz, parts, n_rows):
        self.name = name
        self.nnz = nnz
        self.parts = parts
        self.cols = nnz // parts
        assert self.cols * parts == nnz
        self.groups = -(-self.cols // Q)
        self.bins = -(-n_rows // P)
        self.nb = self.bins + 1
        slots = Q * P + U * self.bins
        self.kblocks = -(-slots // (U * P))
        self.hi = self.kblocks * U
        units = -(-(nnz + (U - 1) * self.groups * self.bins) // U) + self.bins * (P // U - 1)
        self.blocks = -(-units * U // (P * P))
        self.chunks = self.blocks * P
        self.units = self.chunks * P // U


SESSION = EdgeList("sess", NNZ_S, 125, N_SESS)
ADJACENCY = EdgeList("adj", NNZ_A, 128, N_TOTAL)
LISTS = (SESSION, ADJACENCY)
HALF = 8
CHAIN = 8
UB = P * P // U
NC = -(-N_SCORE // 512)
NBC = BATCH // 512
OA, OD = -(-NC // 2), NC // 2
NG = 2 * HALF
TURNS = P // NG
IP, IT = 125, 50
BT = BATCH // P


def build_program(nc, batch_idx, emb, w, bias, sess_vals, a_vals, item_idx, item_emb_idx,
                  sess_rows, sess_cols, a_rows, a_cols, out):
    with ExitStack() as ctx:
        def sb(name, shape, dt):
            return ctx.enter_context(nc.sbuf_tensor(name, shape, dt))

        def ps(name, shape, dt=F32):
            return ctx.enter_context(nc.psum_tensor(name, shape, dt))

        def sem(name):
            return ctx.enter_context(nc.semaphore(name))

        x_rows = nc.dram_tensor("x_rows", (N_TOTAL, D), F32, kind="Internal").ap()
        item_rows = nc.dram_tensor("item_rows", (N_ITEMS, D), F32, kind="Internal").ap()
        h_rows = nc.dram_tensor("h_rows", (ADJACENCY.bins * P, D), F32, kind="Internal").ap()
        records = [nc.dram_tensor(f"rec_{L.name}", (L.units, U * FLD), F32, kind="Internal").ap()
                   for L in LISTS]

        A = ADJACENCY
        COLS = A.groups * Q
        sums = sb("sums", [P, max(A.nb * D, IT * D + N_SCORE)], F32)
        edges = sb("edges", [P, COLS * FLD + COLS], F32)
        fields = edges[:, 0:COLS * FLD]
        bin_of = edges[:, COLS * FLD:]
        store = sb("store", [P, A.groups * A.hi * FLD], F32)
        zeros = sb("zeros", [P, 512], F32)
        onehot_bin = sb("onehot_bin", [P, Q * A.nb], BF16)
        NSLOT = 8
        onehot_lo = sb("onehot_lo", [P, NSLOT * P], F32)
        placed = sb("placed", [P, NSLOT, A.hi * FLD], F32)
        iota_i = sb("iota_i", [P, 1024], I32)
        iota_f = sb("iota_f", [P, 1024], F32)
        part_i = sb("part_i", [P, 1], I32)
        part_f = sb("part_f", [P, 1], F32)
        iota_bf = sb("iota_bf", [P, P], BF16)
        iota_hi = sb("iota_hi", [P, A.hi, FLD], F32)
        rank_mat = sb("rank_mat", [P, P], BF16)
        rank_tmp = sb("rank_tmp", [P, P], F32)
        step = sb("step", [P, 96], BF16)
        sel = sb("sel", [64, Q, P], F32)
        sel_base = sb("sel_base", [64, 1], F32)
        ident = sb("ident", [P, P], F32)
        before = sb("before", [P, P], F32)
        diff = sb("diff", [P, P], F32)
        ones = sb("ones", [P, 1], F32)
        unit_no = sb("unit_no", [P, A.kblocks], F32)
        cnt_i = sb("cnt_i", [64, A.nb], I32)
        cnt8 = sb("cnt8", [64, A.nb], F32)
        incl = sb("incl", [64, A.nb], F32)
        base = sb("base", [64, A.nb], F32)
        pos_f = sb("pos_f", [P, Q], F32)
        pos_i = sb("pos_i", [P, Q], I32)
        tmp_i = sb("tmp_i", [P, Q], I32)
        low_i = sb("low_i", [P, Q], I32)
        pos_lo = sb("pos_lo", [P, Q], F32)
        pos_hi = sb("pos_hi", [P, Q], F32)
        lstart = sb("lstart", [A.nb, A.groups], F32)
        size = sb("size", [A.nb, A.groups], F32)
        gscan = sb("gscan", [A.nb, A.groups], F32)
        delta = sb("delta", [A.nb, A.groups], F32)
        ddelta = sb("ddelta", [A.nb, A.groups], F32)
        tot_i = sb("tot_i", [A.nb, 1], I32)
        tot = sb("tot", [A.nb, 1], F32)
        bstart = sb("bstart", [A.nb, 1], F32)
        cend = sb("cend", [A.nb, 1], F32)
        last_mul = sb("last_mul", [A.nb, 2], F32)
        reached = sb("reached", [A.nb, A.kblocks * P], F32)
        chunk_cmp = sb("chunk_cmp", [A.nb, 512], F32)
        cend_c = sb("cend_c", [A.nb, 1], F32)
        dest = sb("dest", [P, A.groups * A.kblocks], I32)
        st_units = sb("st_units", [P, 2, A.hi * FLD], F32)
        st_dest = sb("st_dest", [P, 2, A.kblocks], I32)
        rec_in = sb("rec_in", [P, P * FLD], F32)
        rc_i = sb("rc_i", [P, P], I32)
        rlo_i = sb("rlo_i", [P, P], I32)
        col_i = sb("col_i", [P, P], I32)
        rlo_f = sb("rlo_f", [P, P], F32)
        val_f = sb("val_f", [P, P], F32)
        st_col = sb("st_col", [P, NG], I32)
        gath = sb("gath", [P, NG, D], F32)
        spread = sb("spread", [P, NG, P], F32)
        w_sb = sb("w_sb", [D, D], F32)
        b_sb = sb("b_sb", [D, 1], F32)
        iidx = sb("iidx", [P, 2, IT], I32)
        bidx = sb("bidx", [P, BT], I32)
        bneg = sb("bneg", [P, IT], I32)

        cnt_ps = ps("cnt_ps", [P, 512])
        col_ps = ps("col_ps", [P, 512])
        rank_ps = [ps(f"rank_ps{i}", [P, 512]) for i in range(2)]
        bin_ps = ps("bin_ps", [P, 512])
        tr_ps = ps("tr_ps", [P, 512])
        sum_ps = [ps(f"sum_ps{i}", [P, 512]) for i in range(2)]

        s_const = sem("s_const")
        s_iota = sem("s_iota")
        s_idx = sem("s_idx")
        s_xg = sem("s_xg")
        s_x = sem("s_x")
        s_raw = [sem(f"s_raw_{L.name}") for L in LISTS]
        s_raw_free = sem("s_raw_free")
        s_zero = sem("s_zero")
        s_zeroed = sem("s_zeroed")
        s_dve = sem("s_dve")
        S = []
        for L in LISTS:
            S.append({k: sem(f"{k}_{L.name}") for k in (
                "onehot", "counted", "base", "ranks", "ranks_read", "places", "placed", "binned", "stored", "chain", "meta_chain",
                "columns", "totals", "starts", "delta", "ddelta", "chunk_cmp", "chunk_bin", "binrow",
                "reached", "dest_ps", "dest", "staged", "rec_in", "transposed", "meta", "meta_used",
                "st_col", "spread", "summed", "added", "sums_out")})
            S[-1]["st_used"] = [sem(f"st_used{h}_{L.name}") for h in range(2)]
            S[-1]["gath"] = [sem(f"gath{k}_{L.name}") for k in range(NG)]
        s_fin = {k: sem("fin_" + k) for k in ("idx", "idx_ok", "w", "item_g", "batch_g", "turned", "turned_act", "turned_dve",
                                              "h", "h_read", "o", "o_read_act", "o_read_dve", "out0", "out1")}
        s_pass = {e: sem("pass_" + e) for e in ("pool", "act", "pe", "dve", "sp")}

        item_g = sums[:, 0:IT * D].rearrange("p (t f) -> p t f", f=D)
        item_flat = edges[:, 0:N_SCORE]
        item_t = item_flat.rearrange("f (p t) -> f p t", t=IT)
        orow = [sums[:, IT * D:IT * D + N_SCORE], store[:, 0:N_SCORE]]
        item_h = sums[:, 0:N_SCORE]
        batch_g = gath
        batch_t = spread[:, :, :].rearrange("p a b -> p (a b)")
        batch_h = onehot_lo
        fin_ps = rank_ps
        out_ps = [cnt_ps, col_ps, bin_ps, tr_ps]

        block = ctx.enter_context(nc.Block())
        raw_in = ((sess_rows, sess_cols, sess_vals), (a_rows, a_cols, a_vals))

        def raw(j, L):
            return sums[0:L.parts, j * A.cols:j * A.cols + L.cols]

        @block.sync
        def _(sp):
            sp.dma_start(iidx[0:IP, 0, :], item_emb_idx.rearrange("(p t) -> p t", t=IT)).then_inc(s_idx, 16)
            sp.dma_start(iidx[0:IP, 1, :], item_idx.rearrange("(p t) -> p t", t=IT)).then_inc(s_fin["idx"], 16)
            sp.dma_start(bidx[:, :], batch_idx.rearrange("(p t) -> p t", t=BT)).then_inc(s_fin["idx"], 16)
            sp.dma_start(w_sb[:, :], w).then_inc(s_fin["w"], 16)
            sp.dma_start(b_sb[:, :], bias.rearrange("(p a) -> p a", a=1)).then_inc(s_fin["w"], 16)
            for n, L in enumerate(LISTS):
                s = S[n]
                if n:
                    sp.wait_ge(S[n - 1]["sums_out"], 32)
                for j, src in enumerate(raw_in[n]):
                    dst = raw(j, L) if j == 2 else raw(j, L).bitcast(I32)
                    sp.dma_start(dst, src.rearrange("(p t) -> p t", t=L.cols)).then_inc(s_raw[n], 16)
                if n == 0:
                    sp.wait_ge(s_zero, 1)
                    for m, M in enumerate(LISTS):
                        for z in range(0, M.blocks, 2):
                            nch = min(2, M.blocks - z)
                            sp.dma_start(records[m][z * UB:(z + nch) * UB, :].rearrange("(p a) f -> p (a f)", p=P),
                                         zeros[:, 0:nch * P * FLD]).then_inc(s_zeroed, 16)
                for h in range(2):
                    sp.wait_ge(s["st_used"][h], 16 * L.kblocks * (L.groups // 2))
                rec_v = records[n].rearrange("(c u) f -> c (u f)", u=P // U)
                with sp.Fori(0, L.blocks) as blk:
                    sp.wait_ge(s["transposed"], blk + 1)
                    sp.dma_start(rec_in[:, :], rec_v[bass.ds(blk * P, P), :]).then_inc(s["rec_in"], 16)
                sp.wait_ge(s["added"], L.chunks + 1)
                if n == 0:
                    full = N_SESS // P
                    rest = N_SESS - full * P
                    sp.dma_start(x_rows[0:full * P, :].rearrange("(b p) f -> p b f", p=P),
                                 sums[:, 0:full * D].rearrange("p (b f) -> p b f", f=D)).then_inc(s["sums_out"], 16)
                    sp.dma_start(x_rows[full * P:N_SESS, :],
                                 sums[0:rest, full * D:(full + 1) * D]).then_inc(s["sums_out"], 16)
                else:
                    half = L.bins // 2
                    for a, b in ((0, half), (half, L.bins)):
                        sp.dma_start(h_rows[a * P:b * P, :].rearrange("(b p) f -> p b f", p=P),
                                     sums[:, a * D:b * D].rearrange("p (b f) -> p b f", f=D)).then_inc(s["sums_out"], 16)
            out_v = out.rearrange("(p t) n -> t p n", t=BT)
            for t in range(BT):
                sp.wait_ge(s_fin["o_read_act"], OA * (t + 1))
                sp.wait_ge(s_fin["o_read_dve"], OD * (t + 1))
                sp.dma_start(out_v[t], orow[t % 2]).then_inc(s_fin[("out0", "out1")[t % 2]], 16)
            for k in ("out0", "out1"):
                sp.wait_ge(s_fin[k], 16 * (BT // 2))

        @block.gpsimd
        def _(pool):
            pool.iota(iota_i[:, :], pattern=[[1, 1024]], base=0, channel_multiplier=0).then_inc(s_iota, 1)
            pool.iota(part_i[:, :], pattern=[[1, 1]], base=0, channel_multiplier=1).then_inc(s_iota, 1)
            pool.memset(zeros[:, :], 0.0).then_inc(s_zero, 1)
            pool.wait_ge(s_idx, 16)
            x_stage = store[0:IP, 0:IT * D].rearrange("p (t f) -> p t f", f=D)
            for t in range(IT):
                pool.indirect_dma_start(x_stage[:, t, :], None, emb,
                                        bass.IndirectOffsetOnAxis(iidx[0:IP, 0, t:t + 1], 0)).then_inc(s_xg, 16)
            pool.wait_ge(s_xg, 16 * IT)
            pool.dma_start(x_rows[N_SESS:N_TOTAL, :].rearrange("(p t) f -> p t f", t=IT), x_stage).then_inc(s_x, 16)
            pool.dma_start(item_rows.rearrange("(p t) f -> p t f", t=IT), x_stage).then_inc(s_x, 16)
            pool.wait_ge(s_x, 32)
            for n, L in enumerate(LISTS):
                s = S[n]
                if n == 0:
                    pool.wait_ge(s_zeroed, 16 * sum(-(-M.blocks // 2) for M in LISTS))
                else:
                    pool.wait_ge(S[0]["sums_out"], 32)
                with pool.Fori(0, L.groups // 2) as i:
                    for h in range(2):
                        pool.wait_ge(s["staged"], i * 2 + h + 1)
                        pool.sem_inc(s_pass["pool"], 1)
                        for k in range(L.kblocks):
                            pool.indirect_dma_start(
                                records[n][:, :], bass.IndirectOffsetOnAxis(st_dest[:, h, k:k + 1], 0),
                                st_units[:, h, k * U * FLD:(k + 1) * U * FLD], None,
                                bounds_check=L.units - 1, oob_is_err=False).then_inc(s["st_used"][h], 16)
                with pool.Fori(0, L.chunks // NG) as i:
                    for h in range(2):
                        pool.wait_ge(s["st_col"], i * 2 + h + 1)
                        pool.sem_inc(s_pass["pool"], 1)
                        for k in range(h * HALF, (h + 1) * HALF):
                            pool.indirect_dma_start(gath[:, k, :], None, item_rows if n == 0 else x_rows,
                                                    bass.IndirectOffsetOnAxis(st_col[:, k:k + 1], 0)
                                                    ).then_inc(s["gath"][k], 16)
            pool.wait_ge(S[1]["sums_out"], 32)
            pool.wait_ge(s_fin["idx_ok"], 1)
            for t in range(IT):
                pool.indirect_dma_start(item_g[0:IP, t, :], None, h_rows,
                                        bass.IndirectOffsetOnAxis(iidx[0:IP, 1, t:t + 1], 0)).then_inc(s_fin["item_g"], 16)
            for t in range(BT):
                pool.indirect_dma_start(batch_g[:, t, :], None, h_rows,
                                        bass.IndirectOffsetOnAxis(bidx[:, t:t + 1], 0)).then_inc(s_fin["batch_g"], 16)

        @block.scalar
        def _(act):
            act.wait_ge(s_x, 32)
            for n, L in enumerate(LISTS):
                s = S[n]
                W2 = L.hi * FLD
                act.sem_inc(s["stored"], 1)
                with act.Fori(0, L.groups) as g:
                    act.wait_ge(s["placed"], g * NQ + (NQ + 2))
                    act.sem_inc(s_pass["act"], 1)
                    act.copy(store[:, bass.ds(g * W2, W2)], bin_ps[:, 0:W2]).then_inc(s["stored"], 1)
                act.wait_ge(s["stored"], L.groups + 1)

                def stage(g, h, used):
                    act.wait_ge(s["dest"], g + 1)
                    act.sem_inc(s_pass["act"], 1)
                    if used is not None:
                        act.wait_ge(s["st_used"][h], used)
                        act.sem_inc(s_pass["act"], 1)
                    act.copy(st_dest[:, h, 0:L.kblocks], dest[:, bass.ds(g * L.kblocks, L.kblocks)])
                    act.copy(st_units[:, h, 0:W2], store[:, bass.ds(g * W2, W2)]).then_inc(s["staged"], 1)

                for h in range(2):
                    stage(h, h, None)
                with act.Fori(1, L.groups // 2) as i:
                    for h in range(2):
                        stage(i * 2 + h, h, i * (16 * L.kblocks))
                with act.Fori(0, L.blocks) as blk:
                    act.wait_ge(s["meta"], blk + 1)
                    act.sem_inc(s_pass["act"], 1)
                    with act.Fori(0, TURNS) as i:
                        for h in range(2):
                            act.wait_ge(s["summed"], (blk * TURNS + i) * 2 + h + 1)
                            act.sem_inc(s_pass["act"], 1)
                            act.copy(st_col[:, h * HALF:(h + 1) * HALF],
                                     col_i[:, bass.ds(i * NG + h * HALF, HALF)]).then_inc(s["st_col"], 1)
                    act.wait_ge(s["st_col"], (blk + 1) * (2 * TURNS))
                    act.sem_inc(s["meta_used"], 1)
            for t in range(0, IT, 2):
                act.wait_ge(s_fin["turned"], t + 1)
                act.copy(item_t[:, :, t], fin_ps[t % 2][:, 0:IP]).then_inc(s_fin["turned_act"], 1)
            act.wait_ge(s_fin["w"], 32)
            for c in range(NC):
                wd = min(512, N_SCORE - c * 512)
                act.wait_ge(s_fin["h"], c + 1)
                act.activation(item_h[:, c * 512:c * 512 + wd], fin_ps[c % 2][:, 0:wd], ACT.Identity,
                               bias=b_sb[:, :]).then_inc(s_fin["h_read"], 1)
            for c in range(NC, NC + NBC):
                act.wait_ge(s_fin["h"], c + 1)
                act.activation(batch_h[:, (c - NC) * 512:(c - NC + 1) * 512], fin_ps[c % 2][:, :], ACT.Identity,
                               bias=b_sb[:, :]).then_inc(s_fin["h_read"], 1)
            for t in range(BT):
                if t >= 2:
                    act.wait_ge(s_fin[("out0", "out1")[t % 2]], 16 * (t // 2))
                for c in range(0, NC, 2):
                    i = t * NC + c
                    wd = min(512, N_SCORE - c * 512)
                    act.wait_ge(s_fin["o"], i + 1)
                    act.copy(orow[t % 2][:, c * 512:c * 512 + wd], out_ps[i % 4][:, 0:wd]).then_inc(s_fin["o_read_act"], 1)

        @block.tensor
        def _(pe):
            pe.wait_ge(s_const, 1)
            for n, L in enumerate(LISTS):
                s = S[n]
                NB = L.nb
                W2 = L.hi * FLD
                with pe.Fori(0, L.groups) as g:
                    for q in range(NQ):
                        pe.wait_ge(s["onehot"], g * NQ + (q + 1))
                        for c in range(q * BATCH_Q, (q + 1) * BATCH_Q):
                            last = nc.tensor.matmul(cnt_ps[0:64, 0:NB], step[:, Q - 1 - c:Q - 1 - c + 64],
                                                    onehot_bin[:, c * NB:(c + 1) * NB],
                                                    start=(c == 0), stop=(c == Q - 1))
                    last.then_inc(s["counted"], 1)
                    pe.wait_ge(s["base"], g + 1)
                    pe.sem_inc(s_pass["pe"], 1)
                    nc.tensor.matmul(col_ps[0:A.nb, bass.ds(g, 1)], base[:, :], sel_base[:, :], start=True, stop=True)
                    nc.tensor.matmul(col_ps[0:A.nb, bass.ds(g + 128, 1)], cnt8[:, :], sel_base[:, :],
                                     start=True, stop=True).then_inc(s["columns"], 1)
                    for q in range(NQ):
                        pe.wait_ge(s["ranks_read"], g * NQ + (q + 1))
                        pe.sem_inc(s_pass["pe"], 1)
                        bank = rank_ps[q % 2]
                        nc.tensor.matmul(bank[:, 0:BATCH_Q * NB], rank_mat[:, :],
                                         onehot_bin[:, q * BATCH_Q * NB:(q + 1) * BATCH_Q * NB],
                                         start=True, stop=False)
                        for c in range(BATCH_Q):
                            last = nc.tensor.matmul(bank[:, c * NB:(c + 1) * NB], sel[:, q * BATCH_Q + c, :],
                                                    base[:, 0:NB], start=False, stop=(c == BATCH_Q - 1))
                        last.then_inc(s["ranks"], 1)
                    pe.wait_ge(s["stored"], g + 1)
                    pe.sem_inc(s_pass["pe"], 1)
                    for q in range(NQ):
                        pe.wait_ge(s["places"], g * NQ + (q + 1))
                        pe.sem_inc(s_pass["pe"], 1)
                        for c in range(q * BATCH_Q, (q + 1) * BATCH_Q):
                            last = nc.tensor.matmul(bin_ps[:, 0:W2], onehot_lo[:, (c % NSLOT) * P:(c % NSLOT + 1) * P],
                                                    placed[:, c % NSLOT, 0:W2], start=(c == 0), stop=(c == Q - 1))
                        last.then_inc(s["placed"], 1)
                pe.wait_ge(s["totals"], 1)
                nc.tensor.matmul(cnt_ps[0:NB, 0:1], before[0:NB, 0:NB], tot[0:NB, :], start=True, stop=True).then_inc(s["starts"], 1)
                pe.wait_ge(s["delta"], 1)
                nc.tensor.matmul(cnt_ps[0:NB, 128:128 + L.groups], diff[0:NB, 0:NB], delta[0:NB, 0:L.groups],
                                 start=True, stop=True).then_inc(s["starts"], 1)
                for c in range(L.chunks // 512 + (L.chunks % 512 > 0)):
                    pe.wait_ge(s["chunk_cmp"], c + 1)
                    nc.tensor.matmul(rank_ps[0][0:1, :], ones[0:L.bins, :], chunk_cmp[0:L.bins, :],
                                     start=True, stop=True).then_inc(s["chunk_bin"], 1)
                with pe.Fori(0, L.groups) as g:
                    pe.wait_ge(s["reached"], g + 1)
                    pe.sem_inc(s_pass["pe"], 1)
                    for k in range(L.kblocks):
                        last = nc.tensor.matmul(cnt_ps[:, k:k + 1], reached[0:NB, k * P:(k + 1) * P],
                                                ddelta[0:NB, bass.ds(g, 1)], start=True, stop=True)
                    last.then_inc(s["dest_ps"], 1)
                pe.sem_inc(s["transposed"], 1)
                pe.sem_inc(s["summed"], 2)
                with pe.Fori(0, L.blocks) as blk:
                    pe.wait_ge(s["rec_in"], (blk + 1) * 16)
                    pe.sem_inc(s_pass["pe"], 1)
                    rec_v = rec_in[:, :].rearrange("c (e f) -> c e f", f=FLD)
                    nc.tensor.transpose(tr_ps[:, 0:P], rec_v[:, :, 0], ident[:, :])
                    nc.tensor.transpose(tr_ps[:, P:2 * P], rec_v[:, :, 1], ident[:, :]).then_inc(s["transposed"], 1)
                    with pe.Fori(0, TURNS) as i:
                        for h in range(2):
                            t = blk * TURNS + i
                            pe.wait_ge(s["spread"], t * 2 + h + 1)
                            pe.sem_inc(s_pass["pe"], 1)
                            pe.wait_ge(s["added"], t * NG + h * HALF + 1)
                            pe.sem_inc(s_pass["pe"], 1)
                            for k in range(h * HALF, (h + 1) * HALF):
                                pe.wait_ge(s["gath"][k], (t + 1) * 16)
                                kk = k - h * HALF
                                last = nc.tensor.matmul(sum_ps[kk // 4][:, (kk % 4) * D:(kk % 4 + 1) * D],
                                                        spread[:, k, :], gath[:, k, :], start=True, stop=True)
                            last.then_inc(s["summed"], 1)
            pe.wait_ge(s_fin["item_g"], 16 * IT)
            for t in range(IT):
                if t >= 2:
                    pe.wait_ge(s_fin[("turned_act", "turned_dve")[t % 2]], t // 2)
                nc.tensor.transpose(fin_ps[t % 2][:, 0:IP], item_g[0:IP, t, :], ident[0:IP, 0:IP]).then_inc(s_fin["turned"], 1)
            pe.wait_ge(s_fin["batch_g"], 16 * BT)
            for t in range(BT):
                nc.tensor.transpose(out_ps[t // 4][:, (t % 4) * P:(t % 4 + 1) * P], batch_g[:, t, :],
                                    ident[:, :]).then_inc(s_fin["turned"], 1)
            pe.wait_ge(s_fin["turned_act"], IT // 2)
            pe.wait_ge(s_fin["turned_dve"], IT // 2 + 2)
            pe.wait_ge(s_fin["w"], 32)
            for c in range(NC + NBC):
                if c >= 2:
                    pe.wait_ge(s_fin["h_read"], c - 1)
                if c < NC:
                    wd = min(512, N_SCORE - c * 512)
                    rhs = item_flat[:, c * 512:c * 512 + wd]
                else:
                    wd = 512
                    rhs = batch_t[:, (c - NC) * 512:(c - NC + 1) * 512]
                nc.tensor.matmul(fin_ps[c % 2][:, 0:wd], w_sb[:, :], rhs, start=True, stop=True).then_inc(s_fin["h"], 1)
            pe.wait_ge(s_fin["h_read"], NC + NBC)
            for t in range(BT):
                for c in range(NC):
                    i = t * NC + c
                    wd = min(512, N_SCORE - c * 512)
                    if i >= 4:
                        tt, cc = divmod(i - 4, NC)
                        done = (OA, OD)[cc % 2] * tt + cc // 2 + 1
                        pe.wait_ge(s_fin[("o_read_act", "o_read_dve")[cc % 2]], done)
                    nc.tensor.matmul(out_ps[i % 4][:, 0:wd], batch_h[:, t * P:(t + 1) * P],
                                     item_h[:, c * 512:c * 512 + wd], start=True, stop=True).then_inc(s_fin["o"], 1)

        @block.vector
        def _(dve):
            chain = [0]

            def link(ins):
                chain[0] += 1
                ins.then_inc(s_dve, 1)
                dve.wait_ge(s_dve, chain[0])

            dve.wait_ge(s_iota, 2)
            link(dve.tensor_copy(part_f[:, :], part_i[:, :]))
            link(dve.tensor_copy(iota_f[:, :], iota_i[:, :]))
            dve.tensor_copy(iota_bf[:, :], iota_f[:, 0:P])
            for f in range(FLD):
                dve.tensor_copy(iota_hi[:, :, f], iota_f[:, 0:A.hi])
            link(dve.tensor_scalar(rank_tmp[:, :], iota_f[:, 0:P], part_f[:, :], OWN, ALU.is_equal, ALU.mult))
            link(dve.scalar_tensor_tensor(rank_mat[:, :], iota_f[:, 0:P], part_f[:, :], rank_tmp[:, :], ALU.is_gt, ALU.add))
            dve.tensor_scalar(ident[:, :], iota_f[:, 0:P], part_f[:, :], None, ALU.is_equal)
            dve.tensor_scalar(before[:, :], iota_f[:, 0:P], part_f[:, :], None, ALU.is_gt)
            link(dve.tensor_scalar(rank_tmp[:, :], iota_f[:, 0:P], -1.0, part_f[:, :], ALU.add, ALU.is_equal))
            dve.scalar_tensor_tensor(diff[:, :], iota_f[:, 0:P], part_f[:, :], rank_tmp[:, :], ALU.is_equal, ALU.subtract)
            dve.tensor_scalar(step[:, :], iota_f[:, 0:96], float(Q), None, ALU.is_ge)
            dve.tensor_scalar(sel_base[:, :], part_f[0:64, :], float(Q), None, ALU.is_equal)
            link(dve.memset(sel[:, :, :], 1.0))
            link(dve.tensor_scalar(sel[:, :, :].rearrange("k c m -> k m c"),
                                   iota_f[0:64, 0:Q].rearrange("k (a c) -> k a c", a=1).broadcast_to([64, P, Q]),
                                   part_f[0:64, :], sel_base[:, :], ALU.is_equal, ALU.add))
            dve.memset(ones[:, :], 1.0)
            for k in range(A.kblocks):
                dve.tensor_scalar(unit_no[:, k:k + 1], part_f[:, :], float(k * P), None, ALU.add)
            dve.memset(cnt8[:, :], 0.0)
            dve.memset(base[:, :], 0.0).then_inc(s_const, 1)
            dve.wait_ge(s_fin["idx"], 32)
            for ix, wdt in ((iidx[0:IP, 1, :], IT), (bidx[:, :], BT)):
                neg = bneg[0:ix.shape[0], 0:wdt]
                link(dve.tensor_scalar(neg, ix, 0.0, float(N_TOTAL), ALU.is_lt, ALU.mult))
                link(dve.tensor_tensor(ix, ix, neg, ALU.add))
                link(dve.tensor_scalar(ix, ix, 0.0, float(N_TOTAL - 1), ALU.max, ALU.min))
            dve.sem_inc(s_fin["idx_ok"], 1)

            for n, L in enumerate(LISTS):
                s = S[n]
                NB = L.nb
                G = L.groups
                W = G * Q
                W2 = L.hi * FLD
                rows_i, cols_i, vals = raw(0, L).bitcast(I32), raw(1, L).bitcast(I32), raw(2, L)
                high_i = raw(3, L).bitcast(I32)
                dve.wait_ge(s_raw[n], 48)
                if n == 0:
                    dve.memset(edges[:, W * FLD:W * FLD + W], -1.0)
                    link(dve.memset(edges[:, 0:W * FLD], 0.0))
                else:
                    dve.memset(edges[:, W * FLD:W * FLD + W], -1.0)
                    link(dve.memset(edges[:, 0:W * FLD], 0.0))
                rec = edges[:, 0:W * FLD].rearrange("p (t f) -> p t f", f=FLD)
                bins = edges[:, W * FLD:W * FLD + W]
                link(dve.tensor_scalar(high_i, rows_i, 7, None, ALU.logical_shift_right))
                link(dve.tensor_copy(bins[0:L.parts, 0:L.cols], high_i))
                link(dve.tensor_scalar(high_i, rows_i, P - 1, COL_BITS, ALU.bitwise_and, ALU.logical_shift_left))
                dve.tensor_tensor(rec[0:L.parts, 0:L.cols, 0], cols_i, high_i, ALU.add)
                link(dve.tensor_copy(rec[0:L.parts, 0:L.cols, 1], vals))
                link(dve.memset(sums[:, 0:NB * D], 0.0))

                dve.sem_inc(s["ranks_read"], 2)
                dve.sem_inc(s["placed"], 2)
                with dve.Fori(0, G) as g:
                    c0 = g * Q
                    for c in range(Q):
                        last = dve.tensor_scalar(onehot_bin[:, c * NB:(c + 1) * NB], iota_bf[:, 0:NB],
                                                 bins[:, bass.ds(c0 + c, 1)], None, ALU.is_equal)
                        if c % BATCH_Q == BATCH_Q - 1:
                            last.then_inc(s["onehot"], 1)
                    dve.wait_ge(s["counted"], g + 1)
                    step_no = [0]

                    def linked(ins):
                        step_no[0] += 1
                        ins.then_inc(s["chain"], 1)
                        dve.wait_ge(s["chain"], g * CHAIN + step_no[0])

                    dve.tensor_copy(base[0:32, 0:NB], cnt_ps[0:32, 0:NB])
                    linked(dve.tensor_scalar(cnt_i[32:64, 0:NB], cnt_ps[32:64, 0:NB], float(U - 1), None, ALU.add))
                    linked(dve.tensor_scalar(cnt_i[32:64, 0:NB], cnt_i[32:64, 0:NB], 3, 3,
                                             ALU.logical_shift_right, ALU.logical_shift_left))
                    linked(dve.tensor_copy(cnt8[32:64, 0:NB], cnt_i[32:64, 0:NB]))
                    linked(dve.tensor_tensor_scan(incl[32:64, 0:NB], cnt8[32:64, 0:NB], cnt8[32:64, 0:NB], 0.0,
                                                  ALU.add, ALU.bypass))
                    dve.tensor_tensor(base[32:64, 0:NB], incl[32:64, 0:NB], cnt8[32:64, 0:NB],
                                      ALU.subtract).then_inc(s["base"], 1)
                    for q in range(NQ):
                        dve.wait_ge(s["ranks"], g * NQ + (q + 1))
                        last = dve.tensor_reduce(pos_f[:, q * BATCH_Q:(q + 1) * BATCH_Q],
                                                 rank_ps[q % 2][:, 0:BATCH_Q * NB].rearrange("p (c b) -> p c b", b=NB),
                                                 AX_X, ALU.max)
                        last.then_inc(s["ranks_read"], 1)
                    dve.wait_ge(s["ranks_read"], g * NQ + (NQ + 2))
                    linked(dve.tensor_scalar(pos_i[:, :], pos_f[:, :], -OWN, None, ALU.add))
                    dve.tensor_scalar(low_i[:, :], pos_i[:, :], 3, P - 1, ALU.arith_shift_right, ALU.bitwise_and)
                    linked(dve.tensor_scalar(tmp_i[:, :], pos_i[:, :], 10, 3, ALU.arith_shift_right, ALU.logical_shift_left))
                    linked(dve.tensor_scalar(pos_i[:, :], pos_i[:, :], U - 1, None, ALU.bitwise_and))
                    dve.tensor_copy(pos_lo[:, :], low_i[:, :])
                    linked(dve.tensor_tensor(pos_hi[:, :], tmp_i[:, :], pos_i[:, :], ALU.add))
                    assert step_no[0] == CHAIN
                    for c in range(Q):
                        k = c % NSLOT
                        if c % BATCH_Q == 0:
                            dve.wait_ge(s["placed"], g * NQ + (c // BATCH_Q + 1))
                        dve.tensor_scalar(onehot_lo[:, k * P:(k + 1) * P], iota_f[:, 0:P], pos_lo[:, c:c + 1], None,
                                          ALU.is_equal)
                        last = dve.scalar_tensor_tensor(
                            placed[:, k, 0:W2].rearrange("p (h f) -> p h f", f=FLD), iota_hi[:, 0:L.hi, :],
                            pos_hi[:, c:c + 1],
                            rec[:, bass.ds(c0 + c, 1), :].broadcast_to([P, L.hi, FLD]), ALU.is_equal, ALU.mult)
                        if c % BATCH_Q == BATCH_Q - 1:
                            last.then_inc(s["places"], 1)
                dve.wait_ge(s["columns"], G)
                dve.tensor_scalar(lstart[0:NB, 0:G], col_ps[0:NB, 0:G], 1.0 / U, None, ALU.mult)
                link(dve.tensor_scalar(size[0:NB, 0:G], col_ps[0:NB, 128:128 + G], 1.0 / U, None, ALU.mult))
                link(dve.tensor_tensor_scan(gscan[0:NB, 0:G], size[0:NB, 0:G], size[0:NB, 0:G], 0.0, ALU.add, ALU.bypass))
                link(dve.tensor_scalar(tot_i[0:NB, :], gscan[0:NB, G - 1:G], float(P // U - 1), None, ALU.add))
                link(dve.tensor_scalar(tot_i[0:NB, :], tot_i[0:NB, :], 4, None, ALU.logical_shift_right))
                dve.tensor_copy(tot[0:NB, :], tot_i[0:NB, :]).then_inc(s["totals"], 1)
                dve.tensor_tensor(delta[0:NB, 0:G], gscan[0:NB, 0:G], size[0:NB, 0:G], ALU.subtract)
                dve.tensor_scalar(last_mul[0:NB, 0:1], part_f[0:NB, :], float(L.bins), None, ALU.not_equal)
                dve.tensor_scalar(last_mul[0:NB, 1:2], part_f[0:NB, :], float(L.bins), FAR, ALU.is_equal, ALU.mult)
                dve.wait_ge(s["starts"], 1)
                link(dve.tensor_scalar(bstart[0:NB, :], cnt_ps[0:NB, 0:1], float(P // U), None, ALU.mult))
                link(dve.tensor_tensor(cend[0:NB, :], cnt_ps[0:NB, 0:1], tot[0:NB, :], ALU.add))
                link(dve.scalar_tensor_tensor(delta[0:NB, 0:G], delta[0:NB, 0:G], bstart[0:NB, :], lstart[0:NB, 0:G],
                                              ALU.add, ALU.subtract))
                dve.tensor_scalar(delta[0:NB, 0:G], delta[0:NB, 0:G], last_mul[0:NB, 0:1], last_mul[0:NB, 1:2],
                                  ALU.mult, ALU.add).then_inc(s["delta"], 1)
                dve.wait_ge(s["starts"], 2)
                link(dve.tensor_copy(ddelta[0:NB, 0:G], cnt_ps[0:NB, 128:128 + G]))
                binrow = edges[0:1, 0:L.chunks].bitcast(I32)
                for c in range(-(-L.chunks // 512)):
                    wd = min(512, L.chunks - c * 512)
                    link(dve.tensor_scalar(cend_c[0:NB, :], cend[0:NB, :], -float(c * 512), None, ALU.add))
                    dve.tensor_scalar(chunk_cmp[0:NB, :], iota_f[0:NB, 0:512], cend_c[0:NB, :], None,
                                      ALU.is_ge).then_inc(s["chunk_cmp"], 1)
                    dve.wait_ge(s["chunk_bin"], c + 1)
                    link(dve.tensor_copy(binrow[:, c * 512:c * 512 + wd], rank_ps[0][0:1, 0:wd]))
                with dve.Fori(0, G) as g:
                    dve.tensor_scalar(reached[0:NB, 0:L.kblocks * P], iota_f[0:NB, 0:L.kblocks * P],
                                      lstart[0:NB, bass.ds(g, 1)], None, ALU.is_ge).then_inc(s["reached"], 1)
                    dve.wait_ge(s["dest_ps"], g + 1)
                    dve.sem_inc(s_pass["dve"], 1)
                    dve.tensor_tensor(dest[:, bass.ds(g * L.kblocks, L.kblocks)], cnt_ps[:, 0:L.kblocks],
                                      unit_no[:, 0:L.kblocks], ALU.add).then_inc(s["dest"], 1)
                dve.sem_inc(s["meta_used"], 1)
                dve.sem_inc(s["added"], 1)
                with dve.Fori(0, L.blocks) as blk:
                    dve.wait_ge(s["transposed"], blk + 2)
                    dve.tensor_copy(rc_i[:, :], tr_ps[:, 0:P]).then_inc(s["meta_chain"], 1)
                    dve.tensor_copy(val_f[:, :], tr_ps[:, P:2 * P])
                    dve.wait_ge(s["meta_used"], blk + 1)
                    dve.sem_inc(s_pass["dve"], 1)
                    dve.wait_ge(s["meta_chain"], blk * 3 + 1)
                    dve.tensor_scalar(rlo_i[:, :], rc_i[:, :], COL_BITS, None,
                                      ALU.logical_shift_right).then_inc(s["meta_chain"], 1)
                    dve.tensor_scalar(col_i[:, :], rc_i[:, :], (1 << COL_BITS) - 1, None,
                                      ALU.bitwise_and).then_inc(s["meta"], 1)
                    dve.wait_ge(s["meta_chain"], blk * 3 + 2)
                    dve.tensor_copy(rlo_f[:, :], rlo_i[:, :]).then_inc(s["meta_chain"], 1)
                    dve.wait_ge(s["meta_chain"], blk * 3 + 3)
                    dve.sem_inc(s_pass["dve"], 1)
                    with dve.Fori(0, TURNS) as i:
                        t = blk * TURNS + i
                        for h in range(2):
                            dve.wait_ge(s["summed"], t * 2 + h + 1)
                            dve.sem_inc(s_pass["dve"], 1)
                            for k in range(h * HALF, (h + 1) * HALF):
                                last = dve.tensor_scalar(spread[:, k, :], iota_f[:, 0:P],
                                                         rlo_f[:, bass.ds(i * NG + k, 1)],
                                                         val_f[:, bass.ds(i * NG + k, 1)], ALU.is_equal, ALU.mult)
                            last.then_inc(s["spread"], 1)
                        for h in range(2):
                            dve.wait_ge(s["summed"], t * 2 + h + 3)
                            dve.sem_inc(s_pass["dve"], 1)
                            for k in range(h * HALF, (h + 1) * HALF):
                                kk = k - h * HALF
                                b = dve.value_load(binrow[0:1, bass.ds(t * NG + k, 1)], min_val=0, max_val=L.bins)
                                dst = sums[:, bass.ds(b * D, D)]
                                dve.wait_ge(s["added"], t * NG + (k + 1))
                                dve.tensor_tensor(dst, dst, sum_ps[kk // 4][:, (kk % 4) * D:(kk % 4 + 1) * D],
                                                  ALU.add).then_inc(s["added"], 1)
                if n == 0:
                    dve.wait_ge(S[0]["sums_out"], 32)
            for t in range(1, IT, 2):
                dve.wait_ge(s_fin["turned"], t + 1)
                dve.tensor_copy(item_t[:, :, t], fin_ps[t % 2][:, 0:IP]).then_inc(s_fin["turned_dve"], 1)
            for c in range(NBC):
                dve.wait_ge(s_fin["turned"], IT + 4 * (c + 1))
                dve.tensor_copy(batch_t[:, c * 512:(c + 1) * 512], out_ps[c][:, :]).then_inc(s_fin["turned_dve"], 1)
            for t in range(BT):
                if t >= 2:
                    dve.wait_ge(s_fin[("out0", "out1")[t % 2]], 16 * (t // 2))
                for c in range(1, NC, 2):
                    i = t * NC + c
                    wd = min(512, N_SCORE - c * 512)
                    dve.wait_ge(s_fin["o"], i + 1)
                    dve.tensor_copy(orow[t % 2][:, c * 512:c * 512 + wd], out_ps[i % 4][:, 0:wd]).then_inc(s_fin["o_read_dve"], 1)


_INS = ["r_batch_idxes", "L0_rec_emb_table", "L0_rec_W", "L0_rec_b", "L0_rec_sess_vals", "L0_rec_A_vals",
        "L0_rec_item_idxes", "L0_rec_item_emb_idxes", "L0_rec_sess_rows", "L0_rec_sess_cols",
        "L0_rec_A_rows", "L0_rec_A_cols"]


def kernel(**inputs):
    import numpy as _np
    import concourse.bacc as _bacc
    from concourse import mybir as _mybir
    from concourse.bass_utils import run_bass_kernel_spmd as _run

    nc = _bacc.Bacc("TRN2", target_bir_lowering=False, num_devices=1)
    arrays, args = {}, []
    for name in _INS:
        a = _np.ascontiguousarray(inputs[name])
        arrays[f"in_{name}_dram"] = a
        args.append(nc.dram_tensor(f"in_{name}_dram", a.shape, _mybir.dt.from_np(a.dtype), kind="ExternalInput").ap())
    out = nc.dram_tensor("out_dram", (BATCH, N_SCORE), F32, kind="ExternalOutput").ap()
    build_program(nc, *args, out)
    r = _run(nc, [arrays], core_ids=[0])
    return r.results[0]["out_dram"]
```

```python
from contextlib import ExitStack

import concourse.bass as bass
from concourse import mybir

F32 = mybir.dt.float32
I32 = mybir.dt.int32
BF16 = mybir.dt.bfloat16
ALU = mybir.AluOpType
ACT = mybir.ActivationFunctionType
AX_X = mybir.AxisListType.X

P = 128
D = 128
N_SESS = 6250
N_ITEMS = 6250
N_TOTAL = N_SESS + N_ITEMS
NNZ_S = 62500
NNZ_A = 400000
BATCH = 1024
N_SCORE = 6250

Q = 32
BATCH_Q = 4
NQ = Q // BATCH_Q
U = 8
FLD = 2
OWN = 8192.0
FAR = float(1 << 20)
COL_BITS = 14


RUN = 2
UPR = RUN * P // U


class EdgeList:

    def __init__(self, name, nnz, parts, n_rows):
        self.name = name
        self.nnz = nnz
        self.parts = parts
        self.cols = nnz // parts
        assert self.cols * parts == nnz
        self.groups = -(-self.cols // Q)
        self.bins = -(-n_rows // P)
        self.nb = self.bins + 1
        slots = Q * P + U * self.bins
        self.kblocks = -(-slots // (U * P))
        self.hi = self.kblocks * U
        units = -(-(nnz + (U - 1) * self.groups * self.bins) // U) + self.bins * (UPR - 1)
        self.blocks = -(-units * U // (P * P))
        self.chunks = self.blocks * P
        self.units = self.chunks * P // U
        assert self.groups % 2 == 0


SESSION = EdgeList("sess", NNZ_S, 125, N_SESS)
ADJACENCY = EdgeList("adj", NNZ_A, 128, N_TOTAL)
LISTS = (SESSION, ADJACENCY)
HALF = 8
CHAIN = 11
UB = P * P // U
NC = -(-N_SCORE // 512)
NBC = BATCH // 512
OA, OD = -(-NC // 2), NC // 2
IOTA = ADJACENCY.kblocks * P
HR = HALF // RUN
NG = 2 * HALF
TURNS = P // NG
IP, IT = 125, 50
BT = BATCH // P


def build_program(nc, batch_idx, emb, w, bias, sess_vals, a_vals, item_idx, item_emb_idx,
                  sess_rows, sess_cols, a_rows, a_cols, out):
    with ExitStack() as ctx:
        def sb(name, shape, dt):
            return ctx.enter_context(nc.sbuf_tensor(name, shape, dt))

        def ps(name, shape, dt=F32):
            return ctx.enter_context(nc.psum_tensor(name, shape, dt))

        def sem(name):
            return ctx.enter_context(nc.semaphore(name))

        x_rows = nc.dram_tensor("x_rows", (N_TOTAL, D), F32, kind="Internal").ap()
        item_rows = nc.dram_tensor("item_rows", (N_ITEMS, D), F32, kind="Internal").ap()
        h_rows = nc.dram_tensor("h_rows", (ADJACENCY.bins * P, D), F32, kind="Internal").ap()
        records = [nc.dram_tensor(f"rec_{L.name}", (L.units + UB, U * FLD), F32, kind="Internal").ap()
                   for L in LISTS]

        A = ADJACENCY
        COLS = (A.groups + 2) * Q
        sums = sb("sums", [P, max(A.nb * D, IT * D + N_SCORE)], F32)
        edges = sb("edges", [P, COLS * FLD + COLS], F32)
        fields = edges[:, 0:COLS * FLD]
        bin_of = edges[:, COLS * FLD:]
        store = sb("store", [P, A.groups * A.hi * FLD], F32)
        zeros = sb("zeros", [P, 512], F32)
        turns_i = sb("turns_i", [1, 2], I32)
        onehot_bin = sb("onehot_bin", [P, 2, Q * A.nb], BF16)
        NSLOT = 8
        onehot_lo = sb("onehot_lo", [P, NSLOT * P], F32)
        placed = sb("placed", [P, Q, P], F32)
        distance = sb("distance", [P, 2, BATCH_Q * P], F32)
        one_col = sb("one_col", [P, 1], F32)
        iota_i = sb("iota_i", [P, IOTA], I32)
        iota_f = sb("iota_f", [P, IOTA], F32)
        part_i = sb("part_i", [P, 1], I32)
        part_f = sb("part_f", [P, 1], F32)
        iota_bf = sb("iota_bf", [P, P], BF16)
        iota_hi = sb("iota_hi", [P, A.hi, FLD], F32)
        rank_mat = sb("rank_mat", [P, P], BF16)
        rank_tmp = sb("rank_tmp", [P, P], F32)
        step = sb("step", [P, 96], BF16)
        sel = sb("sel", [P, Q, P], BF16)
        sel_base = sb("sel_base", [64, 1], F32)
        ident = sb("ident", [P, P], F32)
        before = sb("before", [P, P], F32)
        diff = sb("diff", [P, P], F32)
        ones = sb("ones", [P, 1], F32)
        round_up = sb("round_up", [1, 1], F32)
        unit_no = sb("unit_no", [P, A.kblocks], F32)
        cnt_i = sb("cnt_i", [64, A.nb], I32)
        cnt8 = sb("cnt8", [64, A.nb], F32)
        incl = sb("incl", [64, A.nb], F32)
        base = sb("base", [64, A.nb], F32)
        base_i = sb("base_i", [64, 2, A.nb], I32)
        base_hl = sb("base_hl", [P, A.nb], BF16)
        pos_f = sb("pos_f", [P, Q], F32)
        pos_i = sb("pos_i", [P, Q], I32)
        tmp_i = sb("tmp_i", [P, Q], I32)
        low_i = sb("low_i", [P, Q], I32)
        pos_lo = sb("pos_lo", [P, Q], F32)
        pos_hi = sb("pos_hi", [P, Q], F32)
        lstart = sb("lstart", [A.nb, A.groups], F32)
        size = sb("size", [A.nb, A.groups], F32)
        gscan = sb("gscan", [A.nb, A.groups], F32)
        delta = sb("delta", [A.nb, A.groups], F32)
        ddelta = sb("ddelta", [A.nb, A.groups], F32)
        tot_i = sb("tot_i", [A.nb, 1], I32)
        tot = sb("tot", [A.nb, 1], F32)
        bstart = sb("bstart", [A.nb, 1], F32)
        cend = sb("cend", [A.nb, 1], F32)
        last_mul = sb("last_mul", [A.nb, 2], F32)
        reached = sb("reached", [A.nb, A.kblocks * P], F32)
        chunk_cmp = sb("chunk_cmp", [A.nb, 512], F32)
        ends_i = sb("ends_i", [1, 1], I32)
        cend_c = sb("cend_c", [A.nb, 1], F32)
        dest = sb("dest", [P, A.groups * A.kblocks], I32)
        st_units = sb("st_units", [P, 2, A.hi * FLD], F32)
        st_dest = sb("st_dest", [P, 2, A.kblocks], I32)
        rec_in = sb("rec_in", [P, P * FLD], F32)
        rc_i = sb("rc_i", [P, P], I32)
        rlo_i = sb("rlo_i", [P, P], I32)
        col_i = sb("col_i", [P, 2 * P], I32)
        rlo_f = sb("rlo_f", [P, 2 * P], F32)
        val_f = sb("val_f", [P, 2 * P], F32)
        st_col = sb("st_col", [P, NG], I32)
        gath = sb("gath", [P, NG, D], F32)
        spread = sb("spread", [P, NG, P], F32)
        w_sb = sb("w_sb", [D, D], F32)
        b_sb = sb("b_sb", [D, 1], F32)
        iidx = sb("iidx", [P, 2, IT], I32)
        bidx = sb("bidx", [P, BT], I32)
        bneg = sb("bneg", [P, IT], I32)

        cnt_ps = ps("cnt_ps", [P, 512])
        col_ps = ps("col_ps", [P, 512])
        rank_ps = [ps(f"rank_ps{i}", [P, 512]) for i in range(2)]
        bin_ps = ps("bin_ps", [P, 512])
        tr_ps = ps("tr_ps", [P, 512])
        sum_ps = [ps(f"sum_ps{i}", [P, 512]) for i in range(2)]

        s_const = sem("s_const")
        s_iota = sem("s_iota")
        s_idx = sem("s_idx")
        s_xg = sem("s_xg")
        s_x = sem("s_x")
        s_raw = [sem(f"s_raw_{L.name}") for L in LISTS]
        s_raw_free = sem("s_raw_free")
        s_zero = sem("s_zero")
        s_zeroed = sem("s_zeroed")
        s_dve = sem("s_dve")
        S = []
        for L in LISTS:
            S.append({k: sem(f"{k}_{L.name}") for k in (
                "onehot", "counted", "base", "ranks", "ranks_read", "places", "placed", "binned", "stored", "slots", "distance", "lows", "chain", "meta_chain", "blocks", "done",
                "columns", "totals", "starts", "delta", "ddelta", "chunk_cmp", "chunk_bin", "binrow",
                "reached", "dest_ps", "dest", "staged", "rec_in", "transposed", "meta", "meta_used",
                "st_col", "spread", "summed", "added", "sums_out")})
            S[-1]["st_used"] = [sem(f"st_used{h}_{L.name}") for h in range(2)]
            S[-1]["gath"] = [sem(f"gath{k}_{L.name}") for k in range(NG)]
        s_fin = {k: sem("fin_" + k) for k in ("idx", "idx_ok", "w", "item_g", "batch_g", "turned", "turned_act", "turned_dve",
                                              "h", "h_read", "o", "o_read_act", "o_read_dve", "out0", "out1")}
        s_pass = {e: sem("pass_" + e) for e in ("pool", "act", "pe", "dve", "sp")}

        item_g = sums[:, 0:IT * D].rearrange("p (t f) -> p t f", f=D)
        item_flat = edges[:, 0:N_SCORE]
        item_t = item_flat.rearrange("f (p t) -> f p t", t=IT)
        orow = [sums[:, IT * D:IT * D + N_SCORE], store[:, 0:N_SCORE]]
        item_h = sums[:, 0:N_SCORE]
        batch_g = gath
        batch_t = spread[:, :, :].rearrange("p a b -> p (a b)")
        batch_h = onehot_lo
        fin_ps = rank_ps
        out_ps = [cnt_ps, col_ps, bin_ps, tr_ps]

        block = ctx.enter_context(nc.Block())
        raw_in = ((sess_rows, sess_cols, sess_vals), (a_rows, a_cols, a_vals))

        def raw(j, L):
            return sums[0:L.parts, j * A.cols:j * A.cols + L.cols]

        @block.sync
        def _(sp):
            sp.dma_start(iidx[0:IP, 0, :], item_emb_idx.rearrange("(p t) -> p t", t=IT)).then_inc(s_idx, 16)
            sp.dma_start(iidx[0:IP, 1, :], item_idx.rearrange("(p t) -> p t", t=IT)).then_inc(s_fin["idx"], 16)
            sp.dma_start(bidx[:, :], batch_idx.rearrange("(p t) -> p t", t=BT)).then_inc(s_fin["idx"], 16)
            sp.dma_start(w_sb[:, :], w).then_inc(s_fin["w"], 16)
            sp.dma_start(b_sb[:, :], bias.rearrange("(p a) -> p a", a=1)).then_inc(s_fin["w"], 16)
            for n, L in enumerate(LISTS):
                s = S[n]
                if n:
                    sp.wait_ge(S[n - 1]["sums_out"], 32)
                for j, src in enumerate(raw_in[n]):
                    dst = raw(j, L) if j == 2 else raw(j, L).bitcast(I32)
                    sp.dma_start(dst, src.rearrange("(p t) -> p t", t=L.cols)).then_inc(s_raw[n], 16)
                if n == 0:
                    sp.wait_ge(s_zero, 1)
                    for m, M in enumerate(LISTS):
                        for z in range(0, M.blocks + 1, 2):
                            nch = min(2, M.blocks + 1 - z)
                            sp.dma_start(records[m][z * UB:(z + nch) * UB, :].rearrange("(p a) f -> p (a f)", p=P),
                                         zeros[:, 0:nch * P * FLD]).then_inc(s_zeroed, 16)
                for h in range(2):
                    sp.wait_ge(s["st_used"][h], 16 * L.kblocks * (L.groups // 2))
                rec_v = records[n].rearrange("(c u) f -> c (u f)", u=P // U)
                sp.wait_ge(s["blocks"], 1)
                used = sp.value_load(turns_i[0:1, n:n + 1], min_val=1, max_val=L.blocks)
                with sp.Fori(0, used + 1) as blk:
                    sp.wait_ge(s["transposed"], blk + 1)
                    sp.dma_start(rec_in[:, :], rec_v[bass.ds(blk * P, P), :]).then_inc(s["rec_in"], 16)
                sp.wait_ge(s["done"], 1)
                if n == 0:
                    full = N_SESS // P
                    rest = N_SESS - full * P
                    sp.dma_start(x_rows[0:full * P, :].rearrange("(b p) f -> p b f", p=P),
                                 sums[:, 0:full * D].rearrange("p (b f) -> p b f", f=D)).then_inc(s["sums_out"], 16)
                    sp.dma_start(x_rows[full * P:N_SESS, :],
                                 sums[0:rest, full * D:(full + 1) * D]).then_inc(s["sums_out"], 16)
                else:
                    half = L.bins // 2
                    for a, b in ((0, half), (half, L.bins)):
                        sp.dma_start(h_rows[a * P:b * P, :].rearrange("(b p) f -> p b f", p=P),
                                     sums[:, a * D:b * D].rearrange("p (b f) -> p b f", f=D)).then_inc(s["sums_out"], 16)
            out_v = out.rearrange("(p t) n -> t p n", t=BT)
            for t in range(BT):
                sp.wait_ge(s_fin["o_read_act"], OA * (t + 1))
                sp.wait_ge(s_fin["o_read_dve"], OD * (t + 1))
                sp.dma_start(out_v[t], orow[t % 2]).then_inc(s_fin[("out0", "out1")[t % 2]], 16)
            for k in ("out0", "out1"):
                sp.wait_ge(s_fin[k], 16 * (BT // 2))

        @block.gpsimd
        def _(pool):
            pool.iota(iota_i[:, :], pattern=[[1, IOTA]], base=0, channel_multiplier=0).then_inc(s_iota, 1)
            pool.iota(part_i[:, :], pattern=[[1, 1]], base=0, channel_multiplier=1).then_inc(s_iota, 1)
            pool.memset(zeros[:, :], 0.0).then_inc(s_zero, 1)
            pool.wait_ge(s_idx, 16)
            x_stage = store[0:IP, 0:IT * D].rearrange("p (t f) -> p t f", f=D)
            for t in range(IT):
                pool.indirect_dma_start(x_stage[:, t, :], None, emb,
                                        bass.IndirectOffsetOnAxis(iidx[0:IP, 0, t:t + 1], 0)).then_inc(s_xg, 16)
            pool.wait_ge(s_xg, 16 * IT)
            pool.dma_start(x_rows[N_SESS:N_TOTAL, :].rearrange("(p t) f -> p t f", t=IT), x_stage).then_inc(s_x, 16)
            pool.dma_start(item_rows.rearrange("(p t) f -> p t f", t=IT), x_stage).then_inc(s_x, 16)
            pool.wait_ge(s_x, 32)
            for n, L in enumerate(LISTS):
                s = S[n]
                if n == 0:
                    pool.wait_ge(s_zeroed, 16 * sum(-(-(M.blocks + 1) // 2) for M in LISTS))
                else:
                    pool.wait_ge(S[0]["sums_out"], 32)
                with pool.Fori(0, L.groups // 2) as i:
                    for h in range(2):
                        pool.wait_ge(s["staged"], i * 2 + h + 1)
                        pool.sem_inc(s_pass["pool"], 1)
                        for k in range(L.kblocks):
                            pool.indirect_dma_start(
                                records[n][:, :], bass.IndirectOffsetOnAxis(st_dest[:, h, k:k + 1], 0),
                                st_units[:, h, k * U * FLD:(k + 1) * U * FLD], None,
                                bounds_check=L.units - 1, oob_is_err=False).then_inc(s["st_used"][h], 16)
                pool.wait_ge(s["blocks"], 1)
                used = pool.value_load(turns_i[0:1, n:n + 1], min_val=1, max_val=L.blocks)
                with pool.Fori(0, used * TURNS) as i:
                    for h in range(2):
                        pool.wait_ge(s["st_col"], i * 2 + h + 1)
                        pool.sem_inc(s_pass["pool"], 1)
                        for k in range(h * HALF, (h + 1) * HALF):
                            pool.indirect_dma_start(gath[:, k, :], None, item_rows if n == 0 else x_rows,
                                                    bass.IndirectOffsetOnAxis(st_col[:, k:k + 1], 0)
                                                    ).then_inc(s["gath"][k], 16)
            pool.wait_ge(S[1]["sums_out"], 32)
            pool.wait_ge(s_fin["idx_ok"], 1)
            for t in range(IT):
                pool.indirect_dma_start(item_g[0:IP, t, :], None, h_rows,
                                        bass.IndirectOffsetOnAxis(iidx[0:IP, 1, t:t + 1], 0)).then_inc(s_fin["item_g"], 16)
            for t in range(BT):
                pool.indirect_dma_start(batch_g[:, t, :], None, h_rows,
                                        bass.IndirectOffsetOnAxis(bidx[:, t:t + 1], 0)).then_inc(s_fin["batch_g"], 16)

        @block.scalar
        def _(act):
            act.wait_ge(s_x, 32)
            for n, L in enumerate(LISTS):
                s = S[n]
                W2 = L.hi * FLD
                act.sem_inc(s["stored"], 1)
                act.sem_inc(s["lows"], 2)
                act.wait_ge(s_const, 1)
                with act.Fori(0, L.groups) as g:
                    act.wait_ge(s["slots"], g + 1)
                    act.sem_inc(s_pass["act"], 1)
                    for q in range(NQ):
                        act.wait_ge(s["lows"], g * NQ + (q + 1))
                        act.sem_inc(s_pass["act"], 1)
                        for c in range(BATCH_Q):
                            last = act.activation(distance[:, q % 2, c * P:(c + 1) * P], iota_f[:, 0:P], ACT.Abs,
                                                  bias=pos_lo[:, q * BATCH_Q + c:q * BATCH_Q + c + 1])
                        last.then_inc(s["distance"], 1)
                        act.wait_ge(s["placed"], g * NQ + (q + NQ - 1))
                        act.sem_inc(s_pass["act"], 1)
                        act.wait_ge(s["distance"], g * NQ + (q + 1))
                        act.activation(onehot_lo[:, (q % 2) * BATCH_Q * P:(q % 2 + 1) * BATCH_Q * P],
                                       distance[:, q % 2, :], ACT.Relu, bias=one_col[:, :],
                                       scale=-1.0).then_inc(s["lows"], 1)
                    act.wait_ge(s["placed"], g * NQ + 2 * NQ)
                    act.sem_inc(s_pass["act"], 1)
                    act.copy(store[:, bass.ds(g * W2, W2)], bin_ps[:, 0:W2]).then_inc(s["stored"], 1)
                act.wait_ge(s["stored"], L.groups + 1)

                def stage(g, h, used):
                    act.wait_ge(s["dest"], g + 1)
                    act.sem_inc(s_pass["act"], 1)
                    if used is not None:
                        act.wait_ge(s["st_used"][h], used)
                        act.sem_inc(s_pass["act"], 1)
                    act.copy(st_dest[:, h, 0:L.kblocks], dest[:, bass.ds(g * L.kblocks, L.kblocks)])
                    act.copy(st_units[:, h, 0:W2], store[:, bass.ds(g * W2, W2)]).then_inc(s["staged"], 1)

                for h in range(2):
                    stage(h, h, None)
                with act.Fori(1, L.groups // 2) as i:
                    for h in range(2):
                        stage(i * 2 + h, h, i * (16 * L.kblocks))
                act.wait_ge(s["blocks"], 1)
                used = act.value_load(turns_i[0:1, n:n + 1], min_val=1, max_val=L.blocks)
                with act.Fori(0, used) as blk:
                    act.wait_ge(s["meta"], blk + 1)
                    act.sem_inc(s_pass["act"], 1)
                    with act.Fori(0, TURNS) as i:
                        for h in range(2):
                            act.wait_ge(s["summed"], (blk * TURNS + i) * 2 + h + 1)
                            act.sem_inc(s_pass["act"], 1)
                            act.copy(st_col[:, h * HALF:(h + 1) * HALF],
                                     col_i[:, bass.ds((blk & 1) * P + i * NG + h * HALF, HALF)]).then_inc(s["st_col"], 1)
                    act.wait_ge(s["st_col"], (blk + 1) * (2 * TURNS))
                    act.sem_inc(s["meta_used"], 1)
            for t in range(0, IT, 2):
                act.wait_ge(s_fin["turned"], t + 1)
                act.copy(item_t[:, :, t], fin_ps[t % 2][:, 0:IP]).then_inc(s_fin["turned_act"], 1)
            act.wait_ge(s_fin["w"], 32)
            for c in range(NC):
                wd = min(512, N_SCORE - c * 512)
                act.wait_ge(s_fin["h"], c + 1)
                act.activation(item_h[:, c * 512:c * 512 + wd], fin_ps[c % 2][:, 0:wd], ACT.Identity,
                               bias=b_sb[:, :]).then_inc(s_fin["h_read"], 1)
            for c in range(NC, NC + NBC):
                act.wait_ge(s_fin["h"], c + 1)
                act.activation(batch_h[:, (c - NC) * 512:(c - NC + 1) * 512], fin_ps[c % 2][:, :], ACT.Identity,
                               bias=b_sb[:, :]).then_inc(s_fin["h_read"], 1)
            for t in range(BT):
                if t >= 2:
                    act.wait_ge(s_fin[("out0", "out1")[t % 2]], 16 * (t // 2))
                for c in range(0, NC, 2):
                    i = t * NC + c
                    wd = min(512, N_SCORE - c * 512)
                    act.wait_ge(s_fin["o"], i + 1)
                    act.copy(orow[t % 2][:, c * 512:c * 512 + wd], out_ps[i % 4][:, 0:wd]).then_inc(s_fin["o_read_act"], 1)

        @block.tensor
        def _(pe):
            pe.wait_ge(s_const, 1)
            for n, L in enumerate(LISTS):
                s = S[n]
                NB = L.nb
                W2 = L.hi * FLD

                def count(g, par):
                    for q in range(NQ // 2):
                        pe.wait_ge(s["onehot"], g * (NQ // 2) + (q + 1))
                        for c in range(q * 2 * BATCH_Q, (q + 1) * 2 * BATCH_Q):
                            last = nc.tensor.matmul(cnt_ps[0:64, 0:NB], step[:, Q - 1 - c:Q - 1 - c + 64],
                                                    onehot_bin[:, par, c * NB:(c + 1) * NB],
                                                    start=(c == 0), stop=(c == Q - 1))
                    last.then_inc(s["counted"], 1)

                def ranks(g, par, q):
                    pe.wait_ge(s["ranks_read"], g * NQ + (q + 1))
                    pe.sem_inc(s_pass["pe"], 1)
                    bank = rank_ps[q % 2]
                    nc.tensor.matmul(bank[:, 0:BATCH_Q * NB], rank_mat[:, :],
                                     onehot_bin[:, par, q * BATCH_Q * NB:(q + 1) * BATCH_Q * NB],
                                     start=True, stop=False)
                    for c in range(BATCH_Q):
                        last = nc.tensor.matmul(bank[:, c * NB:(c + 1) * NB], sel[:, q * BATCH_Q + c, :],
                                                base_hl[:, 0:NB], start=False, stop=(c == BATCH_Q - 1))
                    last.then_inc(s["ranks"], 1)

                def columns(g):
                    pe.wait_ge(s["base"], g + 1)
                    pe.sem_inc(s_pass["pe"], 1)
                    nc.tensor.matmul(col_ps[0:A.nb, bass.ds(g, 1)], base[:, :], sel_base[:, :], start=True, stop=True)
                    nc.tensor.matmul(col_ps[0:A.nb, bass.ds(g + 128, 1)], cnt8[:, :], sel_base[:, :],
                                     start=True, stop=True).then_inc(s["columns"], 1)

                def place(g, q):
                    pe.wait_ge(s["places"], g * NQ + (q + 1))
                    pe.sem_inc(s_pass["pe"], 1)
                    pe.wait_ge(s["lows"], g * NQ + (q + 3))
                    pe.sem_inc(s_pass["pe"], 1)
                    for c in range(q * BATCH_Q, (q + 1) * BATCH_Q):
                        last = nc.tensor.matmul(bin_ps[:, 0:P], onehot_lo[:, (c % NSLOT) * P:(c % NSLOT + 1) * P],
                                                placed[:, c, :], start=(c == 0), stop=(c == Q - 1))
                    last.then_inc(s["placed"], 1)

                count(0, 0)
                columns(0)
                for q in range(NQ):
                    ranks(0, 0, q)
                    if q == 1:
                        count(1, 1)
                with pe.Fori(0, L.groups // 2) as i:
                    for par in range(2):
                        g = i * 2 + par
                        pe.wait_ge(s["stored"], g + 1)
                        pe.sem_inc(s_pass["pe"], 1)
                        for q in range(5):
                            place(g, q)
                        columns(g + 1)
                        ranks(g + 1, 1 - par, 0)
                        ranks(g + 1, 1 - par, 1)
                        count(g + 2, par)
                        ranks(g + 1, 1 - par, 2)
                        place(g, 5)
                        ranks(g + 1, 1 - par, 3)
                        place(g, 6)
                        ranks(g + 1, 1 - par, 4)
                        ranks(g + 1, 1 - par, 5)
                        place(g, 7)
                        ranks(g + 1, 1 - par, 6)
                        ranks(g + 1, 1 - par, 7)
                pe.wait_ge(s["totals"], 1)
                nc.tensor.matmul(cnt_ps[0:NB, 0:1], before[0:NB, 0:NB], tot[0:NB, :], start=True, stop=True).then_inc(s["starts"], 1)
                pe.wait_ge(s["delta"], 1)
                nc.tensor.matmul(cnt_ps[0:1, 127:128], tot[0:NB, :], ones[0:NB, :], start=True, stop=False)
                nc.tensor.matmul(cnt_ps[0:1, 127:128], ones[0:1, :], round_up[0:1, :], start=False, stop=True)
                nc.tensor.matmul(cnt_ps[0:NB, 128:128 + L.groups], diff[0:NB, 0:NB], delta[0:NB, 0:L.groups],
                                 start=True, stop=True).then_inc(s["starts"], 1)
                for c in range(-(-L.chunks // RUN // 512)):
                    pe.wait_ge(s["chunk_cmp"], c + 1)
                    nc.tensor.matmul(rank_ps[0][0:1, :], ones[0:L.bins, :], chunk_cmp[0:L.bins, :],
                                     start=True, stop=True).then_inc(s["chunk_bin"], 1)
                with pe.Fori(0, L.groups) as g:
                    pe.wait_ge(s["reached"], g + 1)
                    pe.sem_inc(s_pass["pe"], 1)
                    for k in range(L.kblocks):
                        last = nc.tensor.matmul(cnt_ps[:, k:k + 1], reached[0:NB, k * P:(k + 1) * P],
                                                ddelta[0:NB, bass.ds(g, 1)], start=True, stop=True)
                    last.then_inc(s["dest_ps"], 1)
                pe.sem_inc(s["transposed"], 1)
                pe.sem_inc(s["summed"], 2)
                rec_v = rec_in[:, :].rearrange("c (e f) -> c e f", f=FLD)

                def turn_records(number):
                    pe.wait_ge(s["rec_in"], number * 16)
                    pe.sem_inc(s_pass["pe"], 1)
                    nc.tensor.transpose(tr_ps[:, 0:P], rec_v[:, :, 0], ident[:, :])
                    nc.tensor.transpose(tr_ps[:, P:2 * P], rec_v[:, :, 1], ident[:, :]).then_inc(s["transposed"], 1)

                pe.wait_ge(s["blocks"], 1)
                used = pe.value_load(turns_i[0:1, n:n + 1], min_val=1, max_val=L.blocks)
                turn_records(1)
                with pe.Fori(0, used) as blk:
                    pe.wait_ge(s["meta"], blk + 1)
                    pe.sem_inc(s_pass["pe"], 1)
                    turn_records(blk + 2)
                    with pe.Fori(0, TURNS) as i:
                        for h in range(2):
                            t = blk * TURNS + i
                            pe.wait_ge(s["spread"], t * 2 + h + 1)
                            pe.sem_inc(s_pass["pe"], 1)
                            pe.wait_ge(s["added"], (t * 2 + h) * HR + 1)
                            pe.sem_inc(s_pass["pe"], 1)
                            for k in range(h * HALF, (h + 1) * HALF):
                                pe.wait_ge(s["gath"][k], (t + 1) * 16)
                                r = (k - h * HALF) // RUN
                                last = nc.tensor.matmul(sum_ps[h][:, r * D:(r + 1) * D], spread[:, k, :], gath[:, k, :],
                                                        start=(k % RUN == 0), stop=(k % RUN == RUN - 1))
                            last.then_inc(s["summed"], 1)
            pe.wait_ge(s_fin["item_g"], 16 * IT)
            for t in range(IT):
                if t >= 2:
                    pe.wait_ge(s_fin[("turned_act", "turned_dve")[t % 2]], t // 2)
                nc.tensor.transpose(fin_ps[t % 2][:, 0:IP], item_g[0:IP, t, :], ident[0:IP, 0:IP]).then_inc(s_fin["turned"], 1)
            pe.wait_ge(s_fin["batch_g"], 16 * BT)
            for t in range(BT):
                nc.tensor.transpose(out_ps[t // 4][:, (t % 4) * P:(t % 4 + 1) * P], batch_g[:, t, :],
                                    ident[:, :]).then_inc(s_fin["turned"], 1)
            pe.wait_ge(s_fin["turned_act"], IT // 2)
            pe.wait_ge(s_fin["turned_dve"], IT // 2 + 2)
            pe.wait_ge(s_fin["w"], 32)
            for c in range(NC + NBC):
                if c >= 2:
                    pe.wait_ge(s_fin["h_read"], c - 1)
                if c < NC:
                    wd = min(512, N_SCORE - c * 512)
                    rhs = item_flat[:, c * 512:c * 512 + wd]
                else:
                    wd = 512
                    rhs = batch_t[:, (c - NC) * 512:(c - NC + 1) * 512]
                nc.tensor.matmul(fin_ps[c % 2][:, 0:wd], w_sb[:, :], rhs, start=True, stop=True).then_inc(s_fin["h"], 1)
            pe.wait_ge(s_fin["h_read"], NC + NBC)
            for t in range(BT):
                for c in range(NC):
                    i = t * NC + c
                    wd = min(512, N_SCORE - c * 512)
                    if i >= 4:
                        tt, cc = divmod(i - 4, NC)
                        done = (OA, OD)[cc % 2] * tt + cc // 2 + 1
                        pe.wait_ge(s_fin[("o_read_act", "o_read_dve")[cc % 2]], done)
                    nc.tensor.matmul(out_ps[i % 4][:, 0:wd], batch_h[:, t * P:(t + 1) * P],
                                     item_h[:, c * 512:c * 512 + wd], start=True, stop=True).then_inc(s_fin["o"], 1)

        @block.vector
        def _(dve):
            chain = [0]

            def link(ins):
                chain[0] += 1
                ins.then_inc(s_dve, 1)
                dve.wait_ge(s_dve, chain[0])

            dve.wait_ge(s_iota, 2)
            link(dve.tensor_copy(part_f[:, :], part_i[:, :]))
            link(dve.tensor_copy(iota_f[:, :], iota_i[:, :]))
            dve.tensor_copy(iota_bf[:, :], iota_f[:, 0:P])
            for f in range(FLD):
                dve.tensor_copy(iota_hi[:, :, f], iota_f[:, 0:A.hi])
            link(dve.tensor_scalar(rank_tmp[:, :], iota_f[:, 0:P], part_f[:, :], OWN, ALU.is_equal, ALU.mult))
            link(dve.scalar_tensor_tensor(rank_mat[:, :], iota_f[:, 0:P], part_f[:, :], rank_tmp[:, :], ALU.is_gt, ALU.add))
            dve.tensor_scalar(ident[:, :], iota_f[:, 0:P], part_f[:, :], None, ALU.is_equal)
            dve.tensor_scalar(before[:, :], iota_f[:, 0:P], part_f[:, :], None, ALU.is_gt)
            link(dve.tensor_scalar(rank_tmp[:, :], iota_f[:, 0:P], -1.0, part_f[:, :], ALU.add, ALU.is_equal))
            link(dve.scalar_tensor_tensor(diff[:, :], iota_f[:, 0:P], part_f[:, :], rank_tmp[:, :], ALU.is_equal, ALU.subtract))
            dve.tensor_scalar(step[:, :], iota_f[:, 0:96], float(Q), None, ALU.is_ge)
            link(dve.tensor_scalar(rank_tmp[:, 0:1], part_f[:, :], 64.0, -64.0, ALU.is_ge, ALU.mult))
            link(dve.tensor_tensor(rank_tmp[:, 1:2], part_f[:, :], rank_tmp[:, 0:1], ALU.add))
            link(dve.tensor_scalar(rank_tmp[:, 2:3], rank_tmp[:, 1:2], float(Q), None, ALU.is_equal))
            dve.tensor_copy(sel_base[:, :], rank_tmp[0:64, 2:3])
            link(dve.tensor_scalar(sel[:, :, :].rearrange("k c m -> k m c"),
                                   iota_f[:, 0:Q].rearrange("k (a c) -> k a c", a=1).broadcast_to([P, P, Q]),
                                   rank_tmp[:, 1:2], rank_tmp[:, 2:3], ALU.is_equal, ALU.add))
            dve.memset(placed[:, :, :], 0.0)
            dve.memset(ones[:, :], 1.0)
            dve.memset(one_col[:, :], 1.0)
            dve.memset(round_up[:, :], float(P // RUN - 1))
            for k in range(A.kblocks):
                dve.tensor_scalar(unit_no[:, k:k + 1], part_f[:, :], float(k * P), None, ALU.add)
            dve.memset(cnt8[:, :], 0.0)
            dve.memset(base[:, :], 0.0).then_inc(s_const, 1)
            dve.wait_ge(s_fin["idx"], 32)
            for ix, wdt in ((iidx[0:IP, 1, :], IT), (bidx[:, :], BT)):
                neg = bneg[0:ix.shape[0], 0:wdt]
                link(dve.tensor_scalar(neg, ix, 0.0, float(N_TOTAL), ALU.is_lt, ALU.mult))
                link(dve.tensor_tensor(ix, ix, neg, ALU.add))
                link(dve.tensor_scalar(ix, ix, 0.0, float(N_TOTAL - 1), ALU.max, ALU.min))
            dve.sem_inc(s_fin["idx_ok"], 1)

            for n, L in enumerate(LISTS):
                s = S[n]
                NB = L.nb
                G = L.groups
                W = (G + 2) * Q
                W2 = L.hi * FLD
                rows_i, cols_i, vals = raw(0, L).bitcast(I32), raw(1, L).bitcast(I32), raw(2, L)
                high_i = raw(3, L).bitcast(I32)
                dve.wait_ge(s_raw[n], 48)
                dve.memset(edges[:, W * FLD:W * FLD + W], -1.0)
                link(dve.memset(edges[:, 0:W * FLD], 0.0))
                rec = edges[:, 0:W * FLD].rearrange("p (t f) -> p t f", f=FLD)
                bins = edges[:, W * FLD:W * FLD + W]
                link(dve.tensor_scalar(high_i, rows_i, 7, None, ALU.logical_shift_right))
                link(dve.tensor_copy(bins[0:L.parts, 0:L.cols], high_i))
                link(dve.tensor_scalar(high_i, rows_i, P - 1, COL_BITS, ALU.bitwise_and, ALU.logical_shift_left))
                dve.tensor_tensor(rec[0:L.parts, 0:L.cols, 0], cols_i, high_i, ALU.add)
                link(dve.tensor_copy(rec[0:L.parts, 0:L.cols, 1], vals))
                link(dve.memset(sums[:, 0:NB * D], 0.0))

                dve.sem_inc(s["ranks_read"], 2)
                dve.sem_inc(s["placed"], NQ)

                def onehots(g, par):
                    oh = onehot_bin[:, par, 0:Q * NB].rearrange("p (c b) -> p c b", b=NB)
                    for q in range(NQ // 2):
                        c = q * 2 * BATCH_Q
                        dve.tensor_tensor(
                            oh[:, c:c + 2 * BATCH_Q, :],
                            iota_bf[:, 0:NB].rearrange("p (a b) -> p a b", a=1).broadcast_to([P, 2 * BATCH_Q, NB]),
                            bins[:, bass.ds(g * Q + c, 2 * BATCH_Q)].rearrange("p (c a) -> p c a", a=1).broadcast_to(
                                [P, 2 * BATCH_Q, NB]), ALU.is_equal).then_inc(s["onehot"], 1)

                def linked(ins, value):
                    ins.then_inc(s["chain"], 1)
                    dve.wait_ge(s["chain"], value)

                def first_slots(g):
                    v = g * CHAIN
                    dve.wait_ge(s["counted"], g + 1)
                    dve.tensor_copy(base[0:32, 0:NB], cnt_ps[0:32, 0:NB])
                    linked(dve.tensor_scalar(cnt_i[32:64, 0:NB], cnt_ps[32:64, 0:NB], float(U - 1), None, ALU.add), v + 1)
                    linked(dve.tensor_scalar(cnt_i[32:64, 0:NB], cnt_i[32:64, 0:NB], 3, 3,
                                             ALU.logical_shift_right, ALU.logical_shift_left), v + 2)
                    linked(dve.tensor_copy(cnt8[32:64, 0:NB], cnt_i[32:64, 0:NB]), v + 3)
                    linked(dve.tensor_tensor_scan(incl[32:64, 0:NB], cnt8[32:64, 0:NB], cnt8[32:64, 0:NB], 0.0,
                                                  ALU.add, ALU.bypass), v + 4)
                    linked(dve.tensor_tensor(base[32:64, 0:NB], incl[32:64, 0:NB], cnt8[32:64, 0:NB],
                                             ALU.subtract), v + 5)
                    linked(dve.tensor_copy(base_i[:, 0, 0:NB], base[:, 0:NB]), v + 6)
                    dve.tensor_scalar(base_i[:, 1, 0:NB], base_i[:, 0, 0:NB], 8, 8,
                                      ALU.logical_shift_right, ALU.logical_shift_left)
                    linked(dve.tensor_scalar(base_i[:, 0, 0:NB], base_i[:, 0, 0:NB], 255, None, ALU.bitwise_and), v + 7)
                    dve.tensor_copy(base_hl[0:64, 0:NB], base_i[:, 1, 0:NB])
                    dve.tensor_copy(base_hl[64:128, 0:NB], base_i[:, 0, 0:NB]).then_inc(s["base"], 1)

                def read_ranks(g):
                    for q in range(NQ):
                        dve.wait_ge(s["ranks"], g * NQ + (q + 1))
                        dve.tensor_reduce(pos_f[:, q * BATCH_Q:(q + 1) * BATCH_Q],
                                          rank_ps[q % 2][:, 0:BATCH_Q * NB].rearrange("p (c b) -> p c b", b=NB),
                                          AX_X, ALU.max).then_inc(s["ranks_read"], 1)

                onehots(0, 0)
                first_slots(0)
                onehots(1, 1)
                read_ranks(0)
                with dve.Fori(0, G // 2) as i:
                    for par in range(2):
                        g = i * 2 + par
                        v = g * CHAIN + 7
                        dve.wait_ge(s["ranks_read"], g * NQ + (NQ + 2))
                        linked(dve.tensor_scalar(pos_i[:, :], pos_f[:, :], -OWN, None, ALU.add), v + 1)
                        dve.tensor_scalar(low_i[:, :], pos_i[:, :], 3, P - 1, ALU.arith_shift_right, ALU.bitwise_and)
                        linked(dve.tensor_scalar(tmp_i[:, :], pos_i[:, :], 10, 3,
                                                 ALU.arith_shift_right, ALU.logical_shift_left), v + 2)
                        linked(dve.tensor_scalar(pos_i[:, :], pos_i[:, :], U - 1, None, ALU.bitwise_and), v + 3)
                        dve.wait_ge(s["lows"], g * NQ + 2)
                        dve.sem_inc(s_pass["dve"], 1)
                        dve.tensor_scalar(pos_lo[:, :], low_i[:, :], -1.0, None, ALU.mult).then_inc(s["slots"], 1)
                        linked(dve.tensor_tensor(pos_hi[:, :], tmp_i[:, :], pos_i[:, :], ALU.add), v + 4)
                        for c in range(Q):
                            if c % BATCH_Q == 0:
                                dve.wait_ge(s["placed"], g * NQ + (c // BATCH_Q + 1))
                            last = dve.scalar_tensor_tensor(
                                placed[:, c, 0:W2].rearrange("p (h f) -> p h f", f=FLD), iota_hi[:, 0:L.hi, :],
                                pos_hi[:, c:c + 1],
                                rec[:, bass.ds(g * Q + c, 1), :].broadcast_to([P, L.hi, FLD]), ALU.is_equal, ALU.mult)
                            if c % BATCH_Q == BATCH_Q - 1:
                                last.then_inc(s["places"], 1)
                        first_slots(g + 1)
                        onehots(g + 2, par)
                        read_ranks(g + 1)
                dve.wait_ge(s["columns"], G + 1)
                dve.tensor_scalar(lstart[0:NB, 0:G], col_ps[0:NB, 0:G], 1.0 / U, None, ALU.mult)
                link(dve.tensor_scalar(size[0:NB, 0:G], col_ps[0:NB, 128:128 + G], 1.0 / U, None, ALU.mult))
                link(dve.tensor_tensor_scan(gscan[0:NB, 0:G], size[0:NB, 0:G], size[0:NB, 0:G], 0.0, ALU.add, ALU.bypass))
                link(dve.tensor_scalar(tot_i[0:NB, :], gscan[0:NB, G - 1:G], float(UPR - 1), None, ALU.add))
                link(dve.tensor_scalar(tot_i[0:NB, :], tot_i[0:NB, :], UPR.bit_length() - 1, None, ALU.logical_shift_right))
                dve.tensor_copy(tot[0:NB, :], tot_i[0:NB, :]).then_inc(s["totals"], 1)
                dve.tensor_tensor(delta[0:NB, 0:G], gscan[0:NB, 0:G], size[0:NB, 0:G], ALU.subtract)
                dve.tensor_scalar(last_mul[0:NB, 0:1], part_f[0:NB, :], float(L.bins), None, ALU.not_equal)
                dve.tensor_scalar(last_mul[0:NB, 1:2], part_f[0:NB, :], float(L.bins), FAR, ALU.is_equal, ALU.mult)
                dve.wait_ge(s["starts"], 1)
                link(dve.tensor_scalar(bstart[0:NB, :], cnt_ps[0:NB, 0:1], float(UPR), None, ALU.mult))
                link(dve.tensor_tensor(cend[0:NB, :], cnt_ps[0:NB, 0:1], tot[0:NB, :], ALU.add))
                link(dve.scalar_tensor_tensor(delta[0:NB, 0:G], delta[0:NB, 0:G], bstart[0:NB, :], lstart[0:NB, 0:G],
                                              ALU.add, ALU.subtract))
                dve.tensor_scalar(delta[0:NB, 0:G], delta[0:NB, 0:G], last_mul[0:NB, 0:1], last_mul[0:NB, 1:2],
                                  ALU.mult, ALU.add).then_inc(s["delta"], 1)
                dve.wait_ge(s["starts"], 2)
                link(dve.tensor_copy(ddelta[0:NB, 0:G], cnt_ps[0:NB, 128:128 + G]))
                link(dve.tensor_copy(ends_i[0:1, 0:1], cnt_ps[0:1, 127:128]))
                link(dve.tensor_scalar(ends_i[0:1, 0:1], ends_i[0:1, 0:1], (P // RUN).bit_length() - 1, None, ALU.logical_shift_right))
                link(dve.tensor_scalar(turns_i[0:1, n:n + 1], ends_i[0:1, 0:1], 1.0, None, ALU.max))
                dve.sem_inc(s["blocks"], 1)
                binrow = edges[0:1, 0:L.chunks // RUN].bitcast(I32)
                for c in range(-(-L.chunks // RUN // 512)):
                    wd = min(512, L.chunks // RUN - c * 512)
                    link(dve.tensor_scalar(cend_c[0:NB, :], cend[0:NB, :], -float(c * 512), None, ALU.add))
                    dve.tensor_scalar(chunk_cmp[0:NB, :], iota_f[0:NB, 0:512], cend_c[0:NB, :], None,
                                      ALU.is_ge).then_inc(s["chunk_cmp"], 1)
                    dve.wait_ge(s["chunk_bin"], c + 1)
                    link(dve.tensor_copy(binrow[:, c * 512:c * 512 + wd], rank_ps[0][0:1, 0:wd]))
                with dve.Fori(0, G) as g:
                    dve.tensor_scalar(reached[0:NB, 0:L.kblocks * P], iota_f[0:NB, 0:L.kblocks * P],
                                      lstart[0:NB, bass.ds(g, 1)], None, ALU.is_ge).then_inc(s["reached"], 1)
                    dve.wait_ge(s["dest_ps"], g + 1)
                    dve.sem_inc(s_pass["dve"], 1)
                    dve.tensor_tensor(dest[:, bass.ds(g * L.kblocks, L.kblocks)], cnt_ps[:, 0:L.kblocks],
                                      unit_no[:, 0:L.kblocks], ALU.add).then_inc(s["dest"], 1)
                dve.sem_inc(s["meta_used"], 2)
                dve.sem_inc(s["added"], HR + 1)

                def take_apart(number, par):
                    dve.wait_ge(s["transposed"], number + 1)
                    dve.sem_inc(s_pass["dve"], 1)
                    dve.wait_ge(s["meta_used"], number)
                    dve.sem_inc(s_pass["dve"], 1)
                    dve.tensor_copy(rc_i[:, :], tr_ps[:, 0:P]).then_inc(s["meta_chain"], 1)
                    dve.tensor_copy(val_f[:, bass.ds(par * P, P)], tr_ps[:, P:2 * P])
                    dve.wait_ge(s["meta_chain"], number * 3 - 2)
                    dve.tensor_scalar(rlo_i[:, :], rc_i[:, :], COL_BITS, None,
                                      ALU.logical_shift_right).then_inc(s["meta_chain"], 1)
                    dve.tensor_scalar(col_i[:, bass.ds(par * P, P)], rc_i[:, :], (1 << COL_BITS) - 1, None,
                                      ALU.bitwise_and).then_inc(s["meta"], 1)
                    dve.wait_ge(s["meta_chain"], number * 3 - 1)
                    dve.tensor_copy(rlo_f[:, bass.ds(par * P, P)], rlo_i[:, :]).then_inc(s["meta_chain"], 1)
                    dve.wait_ge(s["meta_chain"], number * 3)
                    dve.sem_inc(s_pass["dve"], 1)

                used = dve.value_load(turns_i[0:1, n:n + 1], min_val=1, max_val=L.blocks)
                take_apart(1, 0)
                with dve.Fori(0, used) as blk:
                    take_apart(blk + 2, (blk + 1) & 1)
                    with dve.Fori(0, TURNS) as i:
                        t = blk * TURNS + i
                        for h in range(2):
                            dve.wait_ge(s["summed"], t * 2 + h + 1)
                            dve.sem_inc(s_pass["dve"], 1)
                            for k in range(h * HALF, (h + 1) * HALF):
                                last = dve.tensor_scalar(spread[:, k, :], iota_f[:, 0:P],
                                                         rlo_f[:, bass.ds((blk & 1) * P + i * NG + k, 1)],
                                                         val_f[:, bass.ds((blk & 1) * P + i * NG + k, 1)], ALU.is_equal, ALU.mult)
                            last.then_inc(s["spread"], 1)
                        for h in range(2):
                            dve.wait_ge(s["summed"], t * 2 + h + 3)
                            dve.sem_inc(s_pass["dve"], 1)
                            for r in range(HR):
                                run = (t * 2 + h) * HR + r
                                b = dve.value_load(binrow[0:1, bass.ds(run, 1)], min_val=0, max_val=L.bins)
                                dst = sums[:, bass.ds(b * D, D)]
                                dve.wait_ge(s["added"], run + (HR + 1))
                                dve.tensor_tensor(dst, dst, sum_ps[h][:, r * D:(r + 1) * D],
                                                  ALU.add).then_inc(s["added"], 1)
                dve.wait_ge(s["added"], used * (P // RUN) + (HR + 1))
                dve.sem_inc(s["done"], 1)
                if n == 0:
                    dve.wait_ge(S[0]["sums_out"], 32)
            for t in range(1, IT, 2):
                dve.wait_ge(s_fin["turned"], t + 1)
                dve.tensor_copy(item_t[:, :, t], fin_ps[t % 2][:, 0:IP]).then_inc(s_fin["turned_dve"], 1)
            for c in range(NBC):
                dve.wait_ge(s_fin["turned"], IT + 4 * (c + 1))
                dve.tensor_copy(batch_t[:, c * 512:(c + 1) * 512], out_ps[c][:, :]).then_inc(s_fin["turned_dve"], 1)
            for t in range(BT):
                if t >= 2:
                    dve.wait_ge(s_fin[("out0", "out1")[t % 2]], 16 * (t // 2))
                for c in range(1, NC, 2):
                    i = t * NC + c
                    wd = min(512, N_SCORE - c * 512)
                    dve.wait_ge(s_fin["o"], i + 1)
                    dve.tensor_copy(orow[t % 2][:, c * 512:c * 512 + wd], out_ps[i % 4][:, 0:wd]).then_inc(s_fin["o_read_dve"], 1)


_INS = ["r_batch_idxes", "L0_rec_emb_table", "L0_rec_W", "L0_rec_b", "L0_rec_sess_vals", "L0_rec_A_vals",
        "L0_rec_item_idxes", "L0_rec_item_emb_idxes", "L0_rec_sess_rows", "L0_rec_sess_cols",
        "L0_rec_A_rows", "L0_rec_A_cols"]


def kernel(**inputs):
    import numpy as _np
    import concourse.bacc as _bacc
    from concourse import mybir as _mybir
    from concourse.bass_utils import run_bass_kernel_spmd as _run

    nc = _bacc.Bacc("TRN2", target_bir_lowering=False, num_devices=1)
    arrays, args = {}, []
    for name in _INS:
        a = _np.ascontiguousarray(inputs[name])
        arrays[f"in_{name}_dram"] = a
        args.append(nc.dram_tensor(f"in_{name}_dram", a.shape, _mybir.dt.from_np(a.dtype), kind="ExternalInput").ap())
    out = nc.dram_tensor("out_dram", (BATCH, N_SCORE), F32, kind="ExternalOutput").ap()
    build_program(nc, *args, out)
    r = _run(nc, [arrays], core_ids=[0])
    return r.results[0]["out_dram"]
```

```python
from contextlib import ExitStack

import concourse.bass as bass
from concourse import mybir

F32 = mybir.dt.float32
I32 = mybir.dt.int32
BF16 = mybir.dt.bfloat16
ALU = mybir.AluOpType
ACT = mybir.ActivationFunctionType
AX_X = mybir.AxisListType.X

P = 128
D = 128
N_SESS = 6250
N_ITEMS = 6250
N_TOTAL = N_SESS + N_ITEMS
NNZ_S = 62500
NNZ_A = 400000
BATCH = 1024
N_SCORE = 6250

Q = 32
BATCH_Q = 4
NQ = Q // BATCH_Q
U = 8
FLD = 2
OWN = 8192.0
FAR = float(1 << 20)
COL_BITS = 14


RUN = 2
UPR = RUN * P // U


class EdgeList:

    def __init__(self, name, nnz, parts, n_rows, filtered):
        self.filtered = filtered
        self.name = name
        self.nnz = nnz
        self.parts = parts
        self.cols = nnz // parts
        assert self.cols * parts == nnz
        self.groups = -(-self.cols // Q)
        self.bins = -(-n_rows // P)
        self.nb = self.bins + 1
        slots = Q * P + U * self.bins
        self.kblocks = -(-slots // (U * P))
        self.hi = self.kblocks * U
        units = -(-(nnz + (U - 1) * self.groups * self.bins) // U) + self.bins * (UPR - 1)
        self.blocks = -(-units * U // (P * P))
        self.chunks = self.blocks * P
        self.units = self.chunks * P // U
        assert self.groups % 2 == 0


SESSION = EdgeList("sess", NNZ_S, 125, N_SESS, False)
ADJACENCY = EdgeList("adj", NNZ_A, 128, N_TOTAL, True)
LISTS = (SESSION, ADJACENCY)
HALF = 8
CHAIN = 11
UB = P * P // U
NC = -(-N_SCORE // 512)
NBC = BATCH // 512
OA, OD = -(-NC // 2), NC // 2
IOTA = ADJACENCY.kblocks * P
HR = HALF // RUN
NG = 2 * HALF
TURNS = P // NG
IP, IT = 125, 50
BT = BATCH // P


def build_program(nc, batch_idx, emb, w, bias, sess_vals, a_vals, item_idx, item_emb_idx,
                  sess_rows, sess_cols, a_rows, a_cols, out):
    with ExitStack() as ctx:
        def sb(name, shape, dt):
            return ctx.enter_context(nc.sbuf_tensor(name, shape, dt))

        def ps(name, shape, dt=F32):
            return ctx.enter_context(nc.psum_tensor(name, shape, dt))

        def sem(name):
            return ctx.enter_context(nc.semaphore(name))

        x_rows = nc.dram_tensor("x_rows", (N_TOTAL, D), F32, kind="Internal").ap()
        item_rows = nc.dram_tensor("item_rows", (N_ITEMS, D), F32, kind="Internal").ap()
        LOW_ROWS = -(-(ADJACENCY.groups + 3) * Q // P) * P
        LOW_BLOCKS = LOW_ROWS // P
        low_rows = nc.dram_tensor("low_rows", (LOW_ROWS, P), BF16, kind="Internal").ap()
        h_rows = nc.dram_tensor("h_rows", (ADJACENCY.bins * P, D), F32, kind="Internal").ap()
        records = [nc.dram_tensor(f"rec_{L.name}", (L.units + UB, U * FLD), F32, kind="Internal").ap()
                   for L in LISTS]

        A = ADJACENCY
        COLS = (A.groups + 2) * Q
        sums = sb("sums", [P, max(A.nb * D, IT * D + N_SCORE)], F32)
        edges = sb("edges", [P, COLS * FLD + COLS], F32)
        fields = edges[:, 0:COLS * FLD]
        bin_of = edges[:, COLS * FLD:]
        store = sb("store", [P, A.groups * A.hi * FLD], F32)
        turns_i = sb("turns_i", [1, 2], I32)
        onehot_bin = sb("onehot_bin", [P, 2, Q * A.nb], BF16)
        NSLOT = 8
        onehot_lo = sb("onehot_lo", [P, NSLOT * P], F32)
        placed = sb("placed", [P, Q, P], F32)
        same_hi = sb("same_hi", [P, 2, Q * A.hi], BF16)
        distance = sb("distance", [P, 2, BATCH_Q * P], BF16)
        low_t = sb("low_t", [P, Q * P], BF16)
        needed = sb("needed", [P, A.nb], BF16)
        idx_hi_i = sb("idx_hi_i", [P, IT + BT], I32)
        idx_lo_i = sb("idx_lo_i", [P, IT + BT], I32)
        idx_hi = sb("idx_hi", [P, IT + BT], F32)
        idx_lo = sb("idx_lo", [P, IT + BT], F32)
        one_col = sb("one_col", [P, 1], F32)
        iota_i = sb("iota_i", [P, IOTA], I32)
        iota_f = sb("iota_f", [P, IOTA], F32)
        part_i = sb("part_i", [P, 1], I32)
        part_f = sb("part_f", [P, 1], F32)
        iota_bf = sb("iota_bf", [P, P], BF16)
        rank_mat = sb("rank_mat", [P, P], BF16)
        rank_tmp = sb("rank_tmp", [P, P], F32)
        step = sb("step", [P, 96], BF16)
        sel = sb("sel", [P, Q, P], BF16)
        sel_base = sb("sel_base", [64, 1], F32)
        ident = sb("ident", [P, P], F32)
        before = sb("before", [P, P], F32)
        diff = sb("diff", [P, P], F32)
        ones = sb("ones", [P, 1], F32)
        round_up = sb("round_up", [1, 1], F32)
        unit_no = sb("unit_no", [P, A.kblocks], F32)
        cnt_i = sb("cnt_i", [64, A.nb], I32)
        cnt8 = sb("cnt8", [64, A.nb], F32)
        incl = sb("incl", [64, A.nb], F32)
        base = sb("base", [64, A.nb], F32)
        base_i = sb("base_i", [64, 2, A.nb], I32)
        base_hl = sb("base_hl", [P, A.nb], BF16)
        pos_f = sb("pos_f", [P, Q], F32)
        pos_i = sb("pos_i", [P, Q], I32)
        tmp_i = sb("tmp_i", [P, Q], I32)
        low_i = sb("low_i", [P, Q], I32)
        pos_lo = sb("pos_lo", [P, 2, Q], BF16)
        pos_hi = sb("pos_hi", [P, Q], BF16)
        lstart = sb("lstart", [A.nb, A.groups], F32)
        size = sb("size", [A.nb, A.groups], F32)
        gscan = sb("gscan", [A.nb, A.groups], F32)
        delta = sb("delta", [A.nb, A.groups], F32)
        ddelta = sb("ddelta", [A.nb, A.groups], F32)
        tot_i = sb("tot_i", [A.nb, 1], I32)
        tot = sb("tot", [A.nb, 1], F32)
        bstart = sb("bstart", [A.nb, 1], F32)
        cend = sb("cend", [A.nb, 1], F32)
        last_mul = sb("last_mul", [A.nb, 2], F32)
        ends_i = sb("ends_i", [1, 1], I32)
        cend_c = sb("cend_c", [A.nb, 1], F32)
        dest = sb("dest", [P, A.groups * A.kblocks], I32)
        st_units = sb("st_units", [P, 2, A.hi * FLD], F32)
        st_dest = sb("st_dest", [P, 2, A.kblocks], I32)
        st_col = sb("st_col", [P, NG], I32)
        gath = sb("gath", [P, NG, D], F32)
        spread = sb("spread", [P, NG, P], F32)
        w_sb = sb("w_sb", [D, D], F32)
        b_sb = sb("b_sb", [D, 1], F32)
        iidx = sb("iidx", [P, 2, IT], I32)
        bidx = sb("bidx", [P, BT], I32)

        cnt_ps = ps("cnt_ps", [P, 512])
        col_ps = ps("col_ps", [P, 512])
        rank_ps = [ps(f"rank_ps{i}", [P, 512]) for i in range(2)]
        bin_ps = ps("bin_ps", [P, 512])
        tr_ps = ps("tr_ps", [P, 512])
        sum_ps = [ps(f"sum_ps{i}", [P, 512]) for i in range(2)]

        s_const = sem("s_const")
        s_iota = sem("s_iota")
        s_idx = sem("s_idx")
        s_xg = sem("s_xg")
        s_x = sem("s_x")
        s_raw = [sem(f"s_raw_{L.name}") for L in LISTS]
        s_raw_free = sem("s_raw_free")
        s_low = {k: sem("low_" + k) for k in ("src", "turned", "copied", "out", "expanded", "masked")}
        s_low_in = [sem(f"low_in{h}") for h in range(2)]
        s_need = {k: sem("need_" + k) for k in ("onehot", "counted", "table")}
        s_zero = sem("s_zero")
        s_zeroed = sem("s_zeroed")
        s_dve = sem("s_dve")
        S = []
        for L in LISTS:
            S.append({k: sem(f"{k}_{L.name}") for k in (
                "onehot", "counted", "base", "ranks", "ranks_read", "places", "his", "abs", "placed", "binned", "stored", "slots", "distance", "lows", "chain", "meta_chain", "blocks", "done",
                "columns", "totals", "starts", "delta", "ddelta", "chunk_cmp", "chunk_bin", "binrow",
                "reached", "dest_ps", "dest", "staged", "rec_in", "transposed", "meta", "meta_used",
                "st_col", "spread", "summed", "added", "sums_out")})
            S[-1]["st_used"] = [sem(f"st_used{h}_{L.name}") for h in range(2)]
            S[-1]["gath"] = [sem(f"gath{k}_{L.name}") for k in range(NG)]
        s_fin = {k: sem("fin_" + k) for k in ("idx", "idx_ok", "w", "item_g", "batch_g", "turned", "turned_act", "turned_dve",
                                              "h", "h_read", "o", "o_read_act", "o_read_dve", "out0", "out1")}
        s_pass = {e: sem("pass_" + e) for e in ("pool", "act", "pe", "dve", "sp")}

        late = placed[:, :, :].rearrange("p a b -> p (a b)")
        rec_in = late[:, 0:2 * P]
        rc_i = late[:, 2 * P:3 * P].bitcast(I32)
        rlo_i = late[:, 3 * P:4 * P].bitcast(I32)
        col_i = late[:, 4 * P:6 * P].bitcast(I32)
        rlo_f = late[:, 6 * P:8 * P]
        val_f = late[:, 8 * P:10 * P]
        chunk_cmp = late[0:A.nb, 10 * P:14 * P]
        reached = late[0:A.nb, 14 * P:(14 + A.kblocks) * P]
        low_all = [gath[:, :, :].rearrange("p a b -> p (a b)").bitcast(BF16),
                   spread[:, :, :].rearrange("p a b -> p (a b)").bitcast(BF16)]
        zeros = low_t[:, 0:1024].bitcast(F32)
        need_lo = onehot_lo[:, 0:4 * P // 2].bitcast(BF16).rearrange("p (a b) -> p a b", b=P)
        need_hi = placed[:, 0:4, :].rearrange("p a b -> p (a b)").bitcast(BF16)[:, 0:4 * A.nb].rearrange(
            "p (a b) -> p a b", b=A.nb)
        mask_ps = [sum_ps[0], sum_ps[1], tr_ps]
        item_g = sums[:, 0:IT * D].rearrange("p (t f) -> p t f", f=D)
        item_flat = edges[:, 0:N_SCORE]
        item_t = item_flat.rearrange("f (p t) -> f p t", t=IT)
        orow = [sums[:, IT * D:IT * D + N_SCORE], store[:, 0:N_SCORE]]
        item_h = sums[:, 0:N_SCORE]
        batch_g = gath
        batch_t = spread[:, :, :].rearrange("p a b -> p (a b)")
        batch_h = onehot_lo
        fin_ps = rank_ps
        out_ps = [cnt_ps, col_ps, bin_ps, tr_ps]

        block = ctx.enter_context(nc.Block())
        raw_in = ((sess_rows, sess_cols, sess_vals), (a_rows, a_cols, a_vals))

        def raw(j, L):
            return sums[0:L.parts, j * A.cols:j * A.cols + L.cols]

        @block.sync
        def _(sp):
            sp.dma_start(iidx[0:IP, 0, :], item_emb_idx.rearrange("(p t) -> p t", t=IT)).then_inc(s_idx, 16)
            sp.dma_start(iidx[0:IP, 1, :], item_idx.rearrange("(p t) -> p t", t=IT)).then_inc(s_fin["idx"], 16)
            sp.dma_start(bidx[:, :], batch_idx.rearrange("(p t) -> p t", t=BT)).then_inc(s_fin["idx"], 16)
            sp.dma_start(w_sb[:, :], w).then_inc(s_fin["w"], 16)
            sp.dma_start(b_sb[:, :], bias.rearrange("(p a) -> p a", a=1)).then_inc(s_fin["w"], 16)
            for n, L in enumerate(LISTS):
                s = S[n]
                if n:
                    sp.wait_ge(S[n - 1]["sums_out"], 32)
                for j, src in enumerate(raw_in[n]):
                    dst = raw(j, L) if j == 2 else raw(j, L).bitcast(I32)
                    sp.dma_start(dst, src.rearrange("(p t) -> p t", t=L.cols)).then_inc(s_raw[n], 16)
                if n == 0:
                    sp.wait_ge(s_zero, 1)
                    for m, M in enumerate(LISTS):
                        for z in range(0, M.blocks + 1, 2):
                            nch = min(2, M.blocks + 1 - z)
                            sp.dma_start(records[m][z * UB:(z + nch) * UB, :].rearrange("(p a) f -> p (a f)", p=P),
                                         zeros[:, 0:nch * P * FLD]).then_inc(s_zeroed, 16)
                if L.filtered:
                    sp.wait_ge(s_low["copied"], -(-LOW_BLOCKS // 4))
                    sp.dma_start(low_rows.rearrange("(b c) p -> c b p", c=P),
                                 low_t[:, 0:LOW_ROWS].rearrange("c (b p) -> c b p", p=P)).then_inc(s_low["out"], 16)
                    sp.wait_ge(s_low["out"], 16)
                    low_v = low_rows.rearrange("(g c) p -> g (c p)", c=Q)

                    def load_low(g, h):
                        sp.wait_ge(s_low["expanded"], g + 1)
                        sp.dma_start(low_all[h], low_v[bass.ds(g, 1), :].broadcast_to([P, Q * P])
                                     ).then_inc(s_low_in[h], 16)

                    with sp.Fori(0, L.groups // 2 + 1) as i:
                        for h in range(2):
                            load_low(i * 2 + h, h)
                    load_low(L.groups + 2, 0)
                for h in range(2):
                    sp.wait_ge(s["st_used"][h], 16 * L.kblocks * (L.groups // 2))
                rec_v = records[n].rearrange("(c u) f -> c (u f)", u=P // U)
                sp.wait_ge(s["blocks"], 1)
                used = sp.value_load(turns_i[0:1, n:n + 1], min_val=1, max_val=L.blocks)
                with sp.Fori(0, used + 1) as blk:
                    sp.wait_ge(s["transposed"], blk + 1)
                    sp.dma_start(rec_in[:, :], rec_v[bass.ds(blk * P, P), :]).then_inc(s["rec_in"], 16)
                sp.wait_ge(s["done"], 1)
                if n == 0:
                    full = N_SESS // P
                    rest = N_SESS - full * P
                    sp.dma_start(x_rows[0:full * P, :].rearrange("(b p) f -> p b f", p=P),
                                 sums[:, 0:full * D].rearrange("p (b f) -> p b f", f=D)).then_inc(s["sums_out"], 16)
                    sp.dma_start(x_rows[full * P:N_SESS, :],
                                 sums[0:rest, full * D:(full + 1) * D]).then_inc(s["sums_out"], 16)
                else:
                    half = L.bins // 2
                    for a, b in ((0, half), (half, L.bins)):
                        sp.dma_start(h_rows[a * P:b * P, :].rearrange("(b p) f -> p b f", p=P),
                                     sums[:, a * D:b * D].rearrange("p (b f) -> p b f", f=D)).then_inc(s["sums_out"], 16)
            out_v = out.rearrange("(p t) n -> t p n", t=BT)
            for t in range(BT):
                sp.wait_ge(s_fin["o_read_act"], OA * (t + 1))
                sp.wait_ge(s_fin["o_read_dve"], OD * (t + 1))
                sp.dma_start(out_v[t], orow[t % 2]).then_inc(s_fin[("out0", "out1")[t % 2]], 16)
            for k in ("out0", "out1"):
                sp.wait_ge(s_fin[k], 16 * (BT // 2))

        @block.gpsimd
        def _(pool):
            pool.iota(iota_i[:, :], pattern=[[1, IOTA]], base=0, channel_multiplier=0).then_inc(s_iota, 1)
            pool.iota(part_i[:, :], pattern=[[1, 1]], base=0, channel_multiplier=1).then_inc(s_iota, 1)
            pool.memset(zeros[:, :], 0.0).then_inc(s_zero, 1)
            pool.wait_ge(s_idx, 16)
            x_stage = store[0:IP, 0:IT * D].rearrange("p (t f) -> p t f", f=D)
            for t in range(IT):
                pool.indirect_dma_start(x_stage[:, t, :], None, emb,
                                        bass.IndirectOffsetOnAxis(iidx[0:IP, 0, t:t + 1], 0)).then_inc(s_xg, 16)
            pool.wait_ge(s_xg, 16 * IT)
            pool.dma_start(x_rows[N_SESS:N_TOTAL, :].rearrange("(p t) f -> p t f", t=IT), x_stage).then_inc(s_x, 16)
            pool.dma_start(item_rows.rearrange("(p t) f -> p t f", t=IT), x_stage).then_inc(s_x, 16)
            pool.wait_ge(s_x, 32)
            for n, L in enumerate(LISTS):
                s = S[n]
                W = (L.groups + 2) * Q
                rec = edges[:, 0:W * FLD].rearrange("p (t f) -> p t f", f=FLD)
                pool.sem_inc(s["placed"], NQ)
                pool.sem_inc(s["places"], 2 * NQ)
                pool.sem_inc(s["distance"], 2 * NQ)
                pool.wait_ge(s_const, 1)

                def distances(g, par, q):
                    pool.wait_ge(s["lows"], g * NQ + (q + 1))
                    pool.sem_inc(s_pass["pool"], 1)
                    pool.tensor_tensor(
                        distance[:, q % 2, :].rearrange("p (c j) -> p c j", j=P),
                        iota_bf[:, :].rearrange("p (c j) -> p c j", c=1).broadcast_to([P, BATCH_Q, P]),
                        pos_lo[:, par, q * BATCH_Q:(q + 1) * BATCH_Q].rearrange("p (c j) -> p c j", j=1).broadcast_to(
                            [P, BATCH_Q, P]), ALU.subtract).then_inc(s["distance"], 1)

                with pool.Fori(0, L.groups // 2) as i:
                    for par in range(2):
                        g = i * 2 + par
                        pool.wait_ge(s["slots"], g + 1)
                        pool.sem_inc(s_pass["pool"], 1)
                        distances(g, par, 0)
                        pool.wait_ge(s["his"], g + 1)
                        pool.sem_inc(s_pass["pool"], 1)
                        for q in range(NQ):
                            pool.wait_ge(s["placed"], g * NQ + (q + 1))
                            pool.sem_inc(s_pass["pool"], 1)
                            c = q * BATCH_Q
                            same = same_hi[:, par, 0:Q * L.hi].rearrange("p (c h) -> p c h", h=L.hi)
                            pool.tensor_tensor(
                                placed[:, c:c + BATCH_Q, 0:L.hi * FLD].rearrange("p c (h f) -> p c h f", f=FLD),
                                same[:, c:c + BATCH_Q, :].rearrange("p c (h f) -> p c h f", f=1).broadcast_to([P, BATCH_Q, L.hi, FLD]),
                                rec[:, bass.ds(g * Q + c, BATCH_Q), :].rearrange("p c (h f) -> p c h f", h=1).broadcast_to([P, BATCH_Q, L.hi, FLD]),
                                ALU.mult).then_inc(s["places"], 1)
                            if q + 1 < NQ:
                                distances(g, par, q + 1)
                if n == 0:
                    pool.wait_ge(s_zeroed, 16 * sum(-(-(M.blocks + 1) // 2) for M in LISTS))
                with pool.Fori(0, L.groups // 2) as i:
                    for h in range(2):
                        pool.wait_ge(s["staged"], i * 2 + h + 1)
                        pool.sem_inc(s_pass["pool"], 1)
                        for k in range(L.kblocks):
                            pool.indirect_dma_start(
                                records[n][:, :], bass.IndirectOffsetOnAxis(st_dest[:, h, k:k + 1], 0),
                                st_units[:, h, k * U * FLD:(k + 1) * U * FLD], None,
                                bounds_check=L.units - 1, oob_is_err=False).then_inc(s["st_used"][h], 16)
                if n:
                    pool.wait_ge(S[0]["sums_out"], 32)
                pool.wait_ge(s["blocks"], 1)
                used = pool.value_load(turns_i[0:1, n:n + 1], min_val=1, max_val=L.blocks)
                with pool.Fori(0, used * TURNS) as i:
                    for h in range(2):
                        pool.wait_ge(s["st_col"], i * 2 + h + 1)
                        pool.sem_inc(s_pass["pool"], 1)
                        for k in range(h * HALF, (h + 1) * HALF):
                            pool.indirect_dma_start(gath[:, k, :], None, item_rows if n == 0 else x_rows,
                                                    bass.IndirectOffsetOnAxis(st_col[:, k:k + 1], 0)
                                                    ).then_inc(s["gath"][k], 16)
            pool.wait_ge(S[1]["sums_out"], 32)
            pool.wait_ge(s_fin["idx_ok"], 1)
            for t in range(IT):
                pool.indirect_dma_start(item_g[0:IP, t, :], None, h_rows,
                                        bass.IndirectOffsetOnAxis(iidx[0:IP, 1, t:t + 1], 0)).then_inc(s_fin["item_g"], 16)
            for t in range(BT):
                pool.indirect_dma_start(batch_g[:, t, :], None, h_rows,
                                        bass.IndirectOffsetOnAxis(bidx[:, t:t + 1], 0)).then_inc(s_fin["batch_g"], 16)

        @block.scalar
        def _(act):
            act.wait_ge(s_x, 32)
            for n, L in enumerate(LISTS):
                s = S[n]
                W2 = L.hi * FLD
                act.sem_inc(s["stored"], 1)
                act.sem_inc(s["lows"], 2)
                act.wait_ge(s_const, 1)
                with act.Fori(0, L.groups) as g:
                    for q in range(NQ):
                        half = distance[:, q % 2, :]
                        act.wait_ge(s["distance"], g * NQ + (q + 1 + 2 * NQ))
                        act.sem_inc(s_pass["act"], 1)
                        act.activation(half, half, ACT.Abs).then_inc(s["abs"], 1)
                        act.wait_ge(s["placed"], g * NQ + (q + NQ - 1))
                        act.sem_inc(s_pass["act"], 1)
                        act.wait_ge(s["abs"], g * NQ + (q + 1))
                        act.activation(onehot_lo[:, (q % 2) * BATCH_Q * P:(q % 2 + 1) * BATCH_Q * P],
                                       half, ACT.Relu, bias=one_col[:, :],
                                       scale=-1.0).then_inc(s["lows"], 1)
                    act.wait_ge(s["placed"], g * NQ + 2 * NQ)
                    act.sem_inc(s_pass["act"], 1)
                    act.copy(store[:, bass.ds(g * W2, W2)], bin_ps[:, 0:W2]).then_inc(s["stored"], 1)
                act.wait_ge(s["stored"], L.groups + 1)

                def stage(g, h, used):
                    act.wait_ge(s["dest"], g + 1)
                    act.sem_inc(s_pass["act"], 1)
                    if used is not None:
                        act.wait_ge(s["st_used"][h], used)
                        act.sem_inc(s_pass["act"], 1)
                    act.copy(st_dest[:, h, 0:L.kblocks], dest[:, bass.ds(g * L.kblocks, L.kblocks)])
                    act.copy(st_units[:, h, 0:W2], store[:, bass.ds(g * W2, W2)]).then_inc(s["staged"], 1)

                for h in range(2):
                    stage(h, h, None)
                with act.Fori(1, L.groups // 2) as i:
                    for h in range(2):
                        stage(i * 2 + h, h, i * (16 * L.kblocks))
                act.wait_ge(s["blocks"], 1)
                used = act.value_load(turns_i[0:1, n:n + 1], min_val=1, max_val=L.blocks)
                with act.Fori(0, used) as blk:
                    act.wait_ge(s["meta"], blk + 1)
                    act.sem_inc(s_pass["act"], 1)
                    with act.Fori(0, TURNS) as i:
                        for h in range(2):
                            act.wait_ge(s["summed"], (blk * TURNS + i) * 2 + h + 1)
                            act.sem_inc(s_pass["act"], 1)
                            act.copy(st_col[:, h * HALF:(h + 1) * HALF],
                                     col_i[:, bass.ds((blk & 1) * P + i * NG + h * HALF, HALF)]).then_inc(s["st_col"], 1)
                    act.wait_ge(s["st_col"], (blk + 1) * (2 * TURNS))
                    act.sem_inc(s["meta_used"], 1)
            for t in range(0, IT, 2):
                act.wait_ge(s_fin["turned"], t + 1)
                act.copy(item_t[:, :, t], fin_ps[t % 2][:, 0:IP]).then_inc(s_fin["turned_act"], 1)
            act.wait_ge(s_fin["w"], 32)
            for c in range(NC):
                wd = min(512, N_SCORE - c * 512)
                act.wait_ge(s_fin["h"], c + 1)
                act.activation(item_h[:, c * 512:c * 512 + wd], fin_ps[c % 2][:, 0:wd], ACT.Identity,
                               bias=b_sb[:, :]).then_inc(s_fin["h_read"], 1)
            for c in range(NC, NC + NBC):
                act.wait_ge(s_fin["h"], c + 1)
                act.activation(batch_h[:, (c - NC) * 512:(c - NC + 1) * 512], fin_ps[c % 2][:, :], ACT.Identity,
                               bias=b_sb[:, :]).then_inc(s_fin["h_read"], 1)
            for t in range(BT):
                if t >= 2:
                    act.wait_ge(s_fin[("out0", "out1")[t % 2]], 16 * (t // 2))
                for c in range(0, NC, 2):
                    i = t * NC + c
                    wd = min(512, N_SCORE - c * 512)
                    act.wait_ge(s_fin["o"], i + 1)
                    act.copy(orow[t % 2][:, c * 512:c * 512 + wd], out_ps[i % 4][:, 0:wd]).then_inc(s_fin["o_read_act"], 1)

        @block.tensor
        def _(pe):
            pe.wait_ge(s_const, 1)
            for n, L in enumerate(LISTS):
                s = S[n]
                NB = L.nb
                W2 = L.hi * FLD

                def mask(g, q):
                    if q == 0:
                        pe.wait_ge(s_low["expanded"], g + 3)
                        pe.sem_inc(s_pass["pe"], 1)
                    for c in range(BATCH_Q):
                        e = (q * BATCH_Q + c) * P
                        last = nc.tensor.matmul(mask_ps[q % 3][:, c * NB:(c + 1) * NB], low_t[:, e:e + P],
                                                needed[:, :], start=True, stop=True)
                    last.then_inc(s_low["masked"], 1)

                def count(g, par, first=0, end=NQ):
                    for q in range(first, end):
                        pe.wait_ge(s["onehot"], g * NQ + (q + 1))
                        if L.filtered and q + 3 < NQ:
                            pe.sem_inc(s_pass["pe"], 1)
                            mask(g, q + 3)
                        for c in range(q * BATCH_Q, (q + 1) * BATCH_Q):
                            last = nc.tensor.matmul(cnt_ps[0:64, 0:NB], step[:, Q - 1 - c:Q - 1 - c + 64],
                                                    onehot_bin[:, par, c * NB:(c + 1) * NB],
                                                    start=(c == 0), stop=(c == Q - 1))
                    if end == NQ:
                        last.then_inc(s["counted"], 1)

                def ranks(g, par, q):
                    pe.wait_ge(s["ranks_read"], g * NQ + (q + 1))
                    pe.sem_inc(s_pass["pe"], 1)
                    bank = rank_ps[q % 2]
                    nc.tensor.matmul(bank[:, 0:BATCH_Q * NB], rank_mat[:, :],
                                     onehot_bin[:, par, q * BATCH_Q * NB:(q + 1) * BATCH_Q * NB],
                                     start=True, stop=False)
                    for c in range(BATCH_Q):
                        last = nc.tensor.matmul(bank[:, c * NB:(c + 1) * NB], sel[:, q * BATCH_Q + c, :],
                                                base_hl[:, 0:NB], start=False, stop=(c == BATCH_Q - 1))
                    last.then_inc(s["ranks"], 1)

                def columns(g):
                    pe.wait_ge(s["base"], g + 1)
                    pe.sem_inc(s_pass["pe"], 1)
                    nc.tensor.matmul(col_ps[0:A.nb, bass.ds(g, 1)], base[:, :], sel_base[:, :], start=True, stop=True)
                    nc.tensor.matmul(col_ps[0:A.nb, bass.ds(g + 128, 1)], cnt8[:, :], sel_base[:, :],
                                     start=True, stop=True).then_inc(s["columns"], 1)

                def place(g, q):
                    pe.wait_ge(s["places"], g * NQ + (q + 1 + 2 * NQ))
                    pe.sem_inc(s_pass["pe"], 1)
                    pe.wait_ge(s["lows"], g * NQ + (q + 3))
                    pe.sem_inc(s_pass["pe"], 1)
                    for c in range(q * BATCH_Q, (q + 1) * BATCH_Q):
                        last = nc.tensor.matmul(bin_ps[:, 0:P], onehot_lo[:, (c % NSLOT) * P:(c % NSLOT + 1) * P],
                                                placed[:, c, :], start=(c == 0), stop=(c == Q - 1))
                    last.then_inc(s["placed"], 1)

                if L.filtered:
                    for j in range(IT + BT):
                        pe.wait_ge(s_need["onehot"], j + 1)
                        np_ = IP if j < IT else P
                        nc.tensor.matmul(bin_ps[:, 0:NB], need_lo[0:np_, j % 4, :], need_hi[0:np_, j % 4, :],
                                         start=(j == 0), stop=(j == IT + BT - 1)).then_inc(s_need["counted"], 1)
                    pe.wait_ge(s_low["src"], 1)
                    for j in range(LOW_BLOCKS):
                        if j >= 8:
                            pe.wait_ge(s_low["copied"], j // 4 - 1)
                        nc.tensor.transpose(sum_ps[j // 4 % 2][:, j % 4 * P:(j % 4 + 1) * P], sums[:, j * P:(j + 1) * P],
                                            ident[:, :]).then_inc(s_low["turned"], 1)
                    pe.wait_ge(s_need["table"], 1)
                    for q in range(3):
                        mask(0, q)
                count(0, 0)
                columns(0)
                for q in range(NQ):
                    ranks(0, 0, q)
                    if q == 1:
                        if L.filtered:
                            for r in range(3):
                                mask(1, r)
                        count(1, 1)
                        if L.filtered:
                            for r in range(3):
                                mask(2, r)
                with pe.Fori(0, L.groups // 2) as i:
                    for par in range(2):
                        g = i * 2 + par
                        columns(g + 1)
                        ranks(g + 1, 1 - par, 0)
                        ranks(g + 1, 1 - par, 1)
                        count(g + 2, par, 0, 1)
                        pe.wait_ge(s["stored"], g + 1)
                        pe.sem_inc(s_pass["pe"], 1)
                        place(g, 0)
                        count(g + 2, par, 1, 4)
                        place(g, 1)
                        count(g + 2, par, 4, NQ)
                        ranks(g + 1, 1 - par, 2)
                        place(g, 2)
                        ranks(g + 1, 1 - par, 3)
                        ranks(g + 1, 1 - par, 4)
                        place(g, 3)
                        for q in range(5, NQ):
                            ranks(g + 1, 1 - par, q)
                        if L.filtered:
                            for q in range(3):
                                mask(g + 3, q)
                        for q in range(4, NQ):
                            place(g, q)
                pe.wait_ge(s["totals"], 1)
                nc.tensor.matmul(cnt_ps[0:NB, 0:1], before[0:NB, 0:NB], tot[0:NB, :], start=True, stop=True).then_inc(s["starts"], 1)
                pe.wait_ge(s["delta"], 1)
                nc.tensor.matmul(cnt_ps[0:1, 127:128], tot[0:NB, :], ones[0:NB, :], start=True, stop=False)
                nc.tensor.matmul(cnt_ps[0:1, 127:128], ones[0:1, :], round_up[0:1, :], start=False, stop=True)
                nc.tensor.matmul(cnt_ps[0:NB, 128:128 + L.groups], diff[0:NB, 0:NB], delta[0:NB, 0:L.groups],
                                 start=True, stop=True).then_inc(s["starts"], 1)
                for c in range(-(-L.chunks // RUN // 512)):
                    pe.wait_ge(s["chunk_cmp"], c + 1)
                    nc.tensor.matmul(rank_ps[0][0:1, :], ones[0:L.bins, :], chunk_cmp[0:L.bins, :],
                                     start=True, stop=True).then_inc(s["chunk_bin"], 1)
                with pe.Fori(0, L.groups) as g:
                    pe.wait_ge(s["reached"], g + 1)
                    pe.sem_inc(s_pass["pe"], 1)
                    for k in range(L.kblocks):
                        last = nc.tensor.matmul(cnt_ps[:, k:k + 1], reached[0:NB, k * P:(k + 1) * P],
                                                ddelta[0:NB, bass.ds(g, 1)], start=True, stop=True)
                    last.then_inc(s["dest_ps"], 1)
                pe.sem_inc(s["transposed"], 1)
                pe.sem_inc(s["summed"], 2)
                rec_v = rec_in[:, :].rearrange("c (e f) -> c e f", f=FLD)

                def turn_records(number):
                    pe.wait_ge(s["rec_in"], number * 16)
                    pe.sem_inc(s_pass["pe"], 1)
                    nc.tensor.transpose(tr_ps[:, 0:P], rec_v[:, :, 0], ident[:, :])
                    nc.tensor.transpose(tr_ps[:, P:2 * P], rec_v[:, :, 1], ident[:, :]).then_inc(s["transposed"], 1)

                pe.wait_ge(s["blocks"], 1)
                used = pe.value_load(turns_i[0:1, n:n + 1], min_val=1, max_val=L.blocks)
                turn_records(1)
                with pe.Fori(0, used) as blk:
                    pe.wait_ge(s["meta"], blk + 1)
                    pe.sem_inc(s_pass["pe"], 1)
                    turn_records(blk + 2)
                    with pe.Fori(0, TURNS) as i:
                        for h in range(2):
                            t = blk * TURNS + i
                            pe.wait_ge(s["spread"], t * 2 + h + 1)
                            pe.sem_inc(s_pass["pe"], 1)
                            pe.wait_ge(s["added"], (t * 2 + h) * HR + 1)
                            pe.sem_inc(s_pass["pe"], 1)
                            for k in range(h * HALF, (h + 1) * HALF):
                                pe.wait_ge(s["gath"][k], (t + 1) * 16)
                                r = (k - h * HALF) // RUN
                                last = nc.tensor.matmul(sum_ps[h][:, r * D:(r + 1) * D], spread[:, k, :], gath[:, k, :],
                                                        start=(k % RUN == 0), stop=(k % RUN == RUN - 1))
                            last.then_inc(s["summed"], 1)
            pe.wait_ge(s_fin["item_g"], 16 * IT)
            for t in range(IT):
                if t >= 2:
                    pe.wait_ge(s_fin[("turned_act", "turned_dve")[t % 2]], t // 2)
                nc.tensor.transpose(fin_ps[t % 2][:, 0:IP], item_g[0:IP, t, :], ident[0:IP, 0:IP]).then_inc(s_fin["turned"], 1)
            pe.wait_ge(s_fin["batch_g"], 16 * BT)
            for t in range(BT):
                nc.tensor.transpose(out_ps[t // 4][:, (t % 4) * P:(t % 4 + 1) * P], batch_g[:, t, :],
                                    ident[:, :]).then_inc(s_fin["turned"], 1)
            pe.wait_ge(s_fin["turned_act"], IT // 2)
            pe.wait_ge(s_fin["turned_dve"], IT // 2 + 2)
            pe.wait_ge(s_fin["w"], 32)
            for c in range(NC + NBC):
                if c >= 2:
                    pe.wait_ge(s_fin["h_read"], c - 1)
                if c < NC:
                    wd = min(512, N_SCORE - c * 512)
                    rhs = item_flat[:, c * 512:c * 512 + wd]
                else:
                    wd = 512
                    rhs = batch_t[:, (c - NC) * 512:(c - NC + 1) * 512]
                nc.tensor.matmul(fin_ps[c % 2][:, 0:wd], w_sb[:, :], rhs, start=True, stop=True).then_inc(s_fin["h"], 1)
            pe.wait_ge(s_fin["h_read"], NC + NBC)
            for t in range(BT):
                for c in range(NC):
                    i = t * NC + c
                    wd = min(512, N_SCORE - c * 512)
                    if i >= 4:
                        tt, cc = divmod(i - 4, NC)
                        done = (OA, OD)[cc % 2] * tt + cc // 2 + 1
                        pe.wait_ge(s_fin[("o_read_act", "o_read_dve")[cc % 2]], done)
                    nc.tensor.matmul(out_ps[i % 4][:, 0:wd], batch_h[:, t * P:(t + 1) * P],
                                     item_h[:, c * 512:c * 512 + wd], start=True, stop=True).then_inc(s_fin["o"], 1)

        @block.vector
        def _(dve):
            chain = [0]

            def link(ins):
                chain[0] += 1
                ins.then_inc(s_dve, 1)
                dve.wait_ge(s_dve, chain[0])

            dve.wait_ge(s_iota, 2)
            link(dve.tensor_copy(part_f[:, :], part_i[:, :]))
            link(dve.tensor_copy(iota_f[:, :], iota_i[:, :]))
            dve.tensor_copy(iota_bf[:, :], iota_f[:, 0:P])
            link(dve.tensor_scalar(rank_tmp[:, :], iota_f[:, 0:P], part_f[:, :], OWN, ALU.is_equal, ALU.mult))
            link(dve.scalar_tensor_tensor(rank_mat[:, :], iota_f[:, 0:P], part_f[:, :], rank_tmp[:, :], ALU.is_gt, ALU.add))
            dve.tensor_scalar(ident[:, :], iota_f[:, 0:P], part_f[:, :], None, ALU.is_equal)
            dve.tensor_scalar(before[:, :], iota_f[:, 0:P], part_f[:, :], None, ALU.is_gt)
            link(dve.tensor_scalar(rank_tmp[:, :], iota_f[:, 0:P], -1.0, part_f[:, :], ALU.add, ALU.is_equal))
            link(dve.scalar_tensor_tensor(diff[:, :], iota_f[:, 0:P], part_f[:, :], rank_tmp[:, :], ALU.is_equal, ALU.subtract))
            dve.tensor_scalar(step[:, :], iota_f[:, 0:96], float(Q), None, ALU.is_ge)
            link(dve.tensor_scalar(rank_tmp[:, 0:1], part_f[:, :], 64.0, -64.0, ALU.is_ge, ALU.mult))
            link(dve.tensor_tensor(rank_tmp[:, 1:2], part_f[:, :], rank_tmp[:, 0:1], ALU.add))
            link(dve.tensor_scalar(rank_tmp[:, 2:3], rank_tmp[:, 1:2], float(Q), None, ALU.is_equal))
            dve.tensor_copy(sel_base[:, :], rank_tmp[0:64, 2:3])
            link(dve.tensor_scalar(sel[:, :, :].rearrange("k c m -> k m c"),
                                   iota_f[:, 0:Q].rearrange("k (a c) -> k a c", a=1).broadcast_to([P, P, Q]),
                                   rank_tmp[:, 1:2], rank_tmp[:, 2:3], ALU.is_equal, ALU.add))
            dve.memset(placed[:, :, :], 0.0)
            dve.memset(ones[:, :], 1.0)
            dve.memset(one_col[:, :], 1.0)
            dve.memset(round_up[:, :], float(P // RUN - 1))
            for k in range(A.kblocks):
                dve.tensor_scalar(unit_no[:, k:k + 1], part_f[:, :], float(k * P), None, ALU.add)
            dve.memset(cnt8[:, :], 0.0)
            dve.memset(base[:, :], 0.0).then_inc(s_const, 1)
            dve.wait_ge(s_fin["idx"], 32)
            for ix, wdt in ((iidx[0:IP, 1, :], IT), (bidx[:, :], BT)):
                neg = rank_tmp[0:ix.shape[0], 0:wdt].bitcast(I32)
                link(dve.tensor_scalar(neg, ix, 0.0, float(N_TOTAL), ALU.is_lt, ALU.mult))
                link(dve.tensor_tensor(ix, ix, neg, ALU.add))
                link(dve.tensor_scalar(ix, ix, 0.0, float(N_TOTAL - 1), ALU.max, ALU.min))
            dve.sem_inc(s_fin["idx_ok"], 1)
            dve.memset(idx_hi_i[:, :], 0)
            link(dve.memset(idx_lo_i[:, :], 0))
            for src, at in ((iidx[0:IP, 1, :], 0), (bidx[:, :], IT)):
                np_, wdt = src.shape
                dve.tensor_scalar(idx_hi_i[0:np_, at:at + wdt], src, 7, None, ALU.logical_shift_right)
                link(dve.tensor_scalar(idx_lo_i[0:np_, at:at + wdt], src, P - 1, None, ALU.bitwise_and))
            dve.tensor_copy(idx_hi[:, :], idx_hi_i[:, :])
            link(dve.tensor_copy(idx_lo[:, :], idx_lo_i[:, :]))

            for n, L in enumerate(LISTS):
                s = S[n]
                NB = L.nb
                G = L.groups
                W = (G + 2) * Q
                W2 = L.hi * FLD
                rows_i, cols_i, vals = raw(0, L).bitcast(I32), raw(1, L).bitcast(I32), raw(2, L)
                high_i = raw(3, L).bitcast(I32)
                dve.wait_ge(s_raw[n], 48)
                dve.memset(edges[:, W * FLD:W * FLD + W], -1.0)
                link(dve.memset(edges[:, 0:W * FLD], 0.0))
                rec = edges[:, 0:W * FLD].rearrange("p (t f) -> p t f", f=FLD)
                bins = edges[:, W * FLD:W * FLD + W]
                link(dve.tensor_scalar(high_i, rows_i, 7, None, ALU.logical_shift_right))
                link(dve.tensor_copy(bins[0:L.parts, 0:L.cols], high_i))
                link(dve.tensor_scalar(high_i, rows_i, P - 1, COL_BITS, ALU.bitwise_and, ALU.logical_shift_left))
                dve.tensor_tensor(rec[0:L.parts, 0:L.cols, 0], cols_i, high_i, ALU.add)
                link(dve.tensor_copy(rec[0:L.parts, 0:L.cols, 1], vals))
                if L.filtered:
                    link(dve.tensor_scalar(high_i, rows_i, P - 1, None, ALU.bitwise_and))
                    dve.memset(sums[:, L.cols:LOW_ROWS], 0.0)
                    dve.tensor_copy(sums[:, 0:L.cols], high_i).then_inc(s_low["src"], 1)
                    for j in range(IT + BT):
                        if j >= 4:
                            dve.wait_ge(s_need["counted"], j - 3)
                        dve.tensor_scalar(need_lo[:, j % 4, :], iota_bf[:, :], idx_lo[:, j:j + 1], None, ALU.is_equal)
                        dve.tensor_scalar(need_hi[:, j % 4, :], iota_bf[:, 0:NB], idx_hi[:, j:j + 1], None,
                                          ALU.is_equal).then_inc(s_need["onehot"], 1)
                    dve.wait_ge(s_need["counted"], IT + BT)
                    link(dve.tensor_scalar(rank_tmp[:, 0:NB], bin_ps[:, 0:NB], 0.0, None, ALU.is_gt))
                    link(dve.scalar_tensor_tensor(rank_tmp[:, 0:NB], iota_f[:, 0:NB], 5.0, rank_tmp[:, 0:NB], ALU.add, ALU.mult))
                    dve.tensor_scalar(needed[:, :], rank_tmp[:, 0:NB], -5.0, None, ALU.add).then_inc(s_need["table"], 1)
                    for j in range(0, LOW_BLOCKS, 4):
                        k = min(4, LOW_BLOCKS - j)
                        dve.wait_ge(s_low["turned"], j + k)
                        dve.tensor_copy(low_t[:, j * P:(j + k) * P], sum_ps[j // 4 % 2][:, 0:k * P]
                                        ).then_inc(s_low["copied"], 1)
                    dve.wait_ge(s_low["out"], 16)
                    dve.sem_inc(s_low["expanded"], 2)
                link(dve.memset(sums[:, 0:NB * D], 0.0))

                dve.sem_inc(s["ranks_read"], 2)

                def expand(number, h):
                    dve.wait_ge(s_low_in[h], number)
                    dve.sem_inc(s_pass["dve"], 1)
                    dve.tensor_scalar(low_t[:, :], low_all[h], part_f[:, :], None,
                                      ALU.is_equal).then_inc(s_low["expanded"], 1)

                def onehots(g, par):
                    oh = onehot_bin[:, par, 0:Q * NB].rearrange("p (c b) -> p c b", b=NB)
                    for q in range(NQ):
                        c = q * BATCH_Q
                        if L.filtered:
                            dve.wait_ge(s_low["masked"], g * NQ + (q + 1))
                            of = mask_ps[q % 3][:, 0:BATCH_Q * NB].rearrange("p (c b) -> p c b", b=NB)
                        else:
                            of = iota_bf[:, 0:NB].rearrange("p (a b) -> p a b", a=1).broadcast_to([P, BATCH_Q, NB])
                        dve.tensor_tensor(
                            oh[:, c:c + BATCH_Q, :], of,
                            bins[:, bass.ds(g * Q + c, BATCH_Q)].rearrange("p (c a) -> p c a", a=1).broadcast_to(
                                [P, BATCH_Q, NB]), ALU.is_equal).then_inc(s["onehot"], 1)

                def linked(ins, value):
                    ins.then_inc(s["chain"], 1)
                    dve.wait_ge(s["chain"], value)

                def first_slots(g):
                    v = g * CHAIN
                    dve.wait_ge(s["counted"], g + 1)
                    dve.tensor_copy(base[0:32, 0:NB], cnt_ps[0:32, 0:NB])
                    linked(dve.tensor_scalar(cnt_i[32:64, 0:NB], cnt_ps[32:64, 0:NB], float(U - 1), None, ALU.add), v + 1)
                    linked(dve.tensor_scalar(cnt_i[32:64, 0:NB], cnt_i[32:64, 0:NB], 3, 3,
                                             ALU.logical_shift_right, ALU.logical_shift_left), v + 2)
                    linked(dve.tensor_copy(cnt8[32:64, 0:NB], cnt_i[32:64, 0:NB]), v + 3)
                    linked(dve.tensor_tensor_scan(incl[32:64, 0:NB], cnt8[32:64, 0:NB], cnt8[32:64, 0:NB], 0.0,
                                                  ALU.add, ALU.bypass), v + 4)
                    linked(dve.tensor_tensor(base[32:64, 0:NB], incl[32:64, 0:NB], cnt8[32:64, 0:NB],
                                             ALU.subtract), v + 5)
                    linked(dve.tensor_copy(base_i[:, 0, 0:NB], base[:, 0:NB]), v + 6)
                    dve.tensor_scalar(base_i[:, 1, 0:NB], base_i[:, 0, 0:NB], 8, 8,
                                      ALU.logical_shift_right, ALU.logical_shift_left)
                    linked(dve.tensor_scalar(base_i[:, 0, 0:NB], base_i[:, 0, 0:NB], 255, None, ALU.bitwise_and), v + 7)
                    dve.tensor_copy(base_hl[0:64, 0:NB], base_i[:, 1, 0:NB])
                    dve.tensor_copy(base_hl[64:128, 0:NB], base_i[:, 0, 0:NB]).then_inc(s["base"], 1)

                def read_ranks(g):
                    for q in range(NQ):
                        dve.wait_ge(s["ranks"], g * NQ + (q + 1))
                        dve.tensor_reduce(pos_f[:, q * BATCH_Q:(q + 1) * BATCH_Q],
                                          rank_ps[q % 2][:, 0:BATCH_Q * NB].rearrange("p (c b) -> p c b", b=NB),
                                          AX_X, ALU.max).then_inc(s["ranks_read"], 1)

                if L.filtered:
                    expand(16, 0)
                onehots(0, 0)
                first_slots(0)
                if L.filtered:
                    expand(16, 1)
                onehots(1, 1)
                if L.filtered:
                    expand(32, 0)
                read_ranks(0)
                with dve.Fori(0, G // 2) as i:
                    for par in range(2):
                        g = i * 2 + par
                        v = g * CHAIN + 7
                        dve.wait_ge(s["ranks_read"], g * NQ + (NQ + 2))
                        linked(dve.tensor_scalar(pos_i[:, :], pos_f[:, :], -OWN, None, ALU.add), v + 1)
                        dve.tensor_scalar(low_i[:, :], pos_i[:, :], 3, P - 1, ALU.arith_shift_right, ALU.bitwise_and)
                        linked(dve.tensor_scalar(tmp_i[:, :], pos_i[:, :], 10, 3,
                                                 ALU.arith_shift_right, ALU.logical_shift_left), v + 2)
                        linked(dve.tensor_scalar(pos_i[:, :], pos_i[:, :], U - 1, None, ALU.bitwise_and), v + 3)
                        dve.wait_ge(s["distance"], g * NQ + NQ)
                        dve.sem_inc(s_pass["dve"], 1)
                        dve.tensor_copy(pos_lo[:, par, :], low_i[:, :]).then_inc(s["slots"], 1)
                        linked(dve.tensor_tensor(pos_hi[:, :], tmp_i[:, :], pos_i[:, :], ALU.add), v + 4)
                        dve.wait_ge(s["places"], g * NQ + NQ)
                        dve.sem_inc(s_pass["dve"], 1)
                        dve.tensor_tensor(
                            same_hi[:, par, 0:Q * L.hi].rearrange("p (c h) -> p c h", h=L.hi),
                            iota_bf[:, 0:L.hi].rearrange("p (c h) -> p c h", c=1).broadcast_to([P, Q, L.hi]),
                            pos_hi[:, :].rearrange("p (c h) -> p c h", h=1).broadcast_to([P, Q, L.hi]),
                            ALU.is_equal).then_inc(s["his"], 1)
                        first_slots(g + 1)
                        onehots(g + 2, par)
                        if L.filtered:
                            expand(i * 16 + (32, 48)[par], 1 - par)
                        read_ranks(g + 1)
                dve.wait_ge(s["columns"], G + 1)
                dve.tensor_scalar(lstart[0:NB, 0:G], col_ps[0:NB, 0:G], 1.0 / U, None, ALU.mult)
                link(dve.tensor_scalar(size[0:NB, 0:G], col_ps[0:NB, 128:128 + G], 1.0 / U, None, ALU.mult))
                link(dve.tensor_tensor_scan(gscan[0:NB, 0:G], size[0:NB, 0:G], size[0:NB, 0:G], 0.0, ALU.add, ALU.bypass))
                link(dve.tensor_scalar(tot_i[0:NB, :], gscan[0:NB, G - 1:G], float(UPR - 1), None, ALU.add))
                link(dve.tensor_scalar(tot_i[0:NB, :], tot_i[0:NB, :], UPR.bit_length() - 1, None, ALU.logical_shift_right))
                dve.tensor_copy(tot[0:NB, :], tot_i[0:NB, :]).then_inc(s["totals"], 1)
                dve.tensor_tensor(delta[0:NB, 0:G], gscan[0:NB, 0:G], size[0:NB, 0:G], ALU.subtract)
                dve.tensor_scalar(last_mul[0:NB, 0:1], part_f[0:NB, :], float(L.bins), None, ALU.not_equal)
                dve.tensor_scalar(last_mul[0:NB, 1:2], part_f[0:NB, :], float(L.bins), FAR, ALU.is_equal, ALU.mult)
                dve.wait_ge(s["starts"], 1)
                link(dve.tensor_scalar(bstart[0:NB, :], cnt_ps[0:NB, 0:1], float(UPR), None, ALU.mult))
                link(dve.tensor_tensor(cend[0:NB, :], cnt_ps[0:NB, 0:1], tot[0:NB, :], ALU.add))
                link(dve.scalar_tensor_tensor(delta[0:NB, 0:G], delta[0:NB, 0:G], bstart[0:NB, :], lstart[0:NB, 0:G],
                                              ALU.add, ALU.subtract))
                dve.tensor_scalar(delta[0:NB, 0:G], delta[0:NB, 0:G], last_mul[0:NB, 0:1], last_mul[0:NB, 1:2],
                                  ALU.mult, ALU.add).then_inc(s["delta"], 1)
                dve.wait_ge(s["starts"], 2)
                link(dve.tensor_copy(ddelta[0:NB, 0:G], cnt_ps[0:NB, 128:128 + G]))
                link(dve.tensor_copy(ends_i[0:1, 0:1], cnt_ps[0:1, 127:128]))
                link(dve.tensor_scalar(ends_i[0:1, 0:1], ends_i[0:1, 0:1], (P // RUN).bit_length() - 1, None, ALU.logical_shift_right))
                link(dve.tensor_scalar(turns_i[0:1, n:n + 1], ends_i[0:1, 0:1], 1.0, None, ALU.max))
                dve.sem_inc(s["blocks"], 1)
                binrow = edges[0:1, 0:L.chunks // RUN].bitcast(I32)
                for c in range(-(-L.chunks // RUN // 512)):
                    wd = min(512, L.chunks // RUN - c * 512)
                    link(dve.tensor_scalar(cend_c[0:NB, :], cend[0:NB, :], -float(c * 512), None, ALU.add))
                    dve.tensor_scalar(chunk_cmp[0:NB, :], iota_f[0:NB, 0:512], cend_c[0:NB, :], None,
                                      ALU.is_ge).then_inc(s["chunk_cmp"], 1)
                    dve.wait_ge(s["chunk_bin"], c + 1)
                    link(dve.tensor_copy(binrow[:, c * 512:c * 512 + wd], rank_ps[0][0:1, 0:wd]))
                with dve.Fori(0, G) as g:
                    dve.tensor_scalar(reached[0:NB, 0:L.kblocks * P], iota_f[0:NB, 0:L.kblocks * P],
                                      lstart[0:NB, bass.ds(g, 1)], None, ALU.is_ge).then_inc(s["reached"], 1)
                    dve.wait_ge(s["dest_ps"], g + 1)
                    dve.sem_inc(s_pass["dve"], 1)
                    dve.tensor_tensor(dest[:, bass.ds(g * L.kblocks, L.kblocks)], cnt_ps[:, 0:L.kblocks],
                                      unit_no[:, 0:L.kblocks], ALU.add).then_inc(s["dest"], 1)
                dve.sem_inc(s["meta_used"], 2)
                dve.sem_inc(s["added"], HR + 1)

                def take_apart(number, par):
                    dve.wait_ge(s["transposed"], number + 1)
                    dve.sem_inc(s_pass["dve"], 1)
                    dve.wait_ge(s["meta_used"], number)
                    dve.sem_inc(s_pass["dve"], 1)
                    dve.tensor_copy(rc_i[:, :], tr_ps[:, 0:P]).then_inc(s["meta_chain"], 1)
                    dve.tensor_copy(val_f[:, bass.ds(par * P, P)], tr_ps[:, P:2 * P])
                    dve.wait_ge(s["meta_chain"], number * 3 - 2)
                    dve.tensor_scalar(rlo_i[:, :], rc_i[:, :], COL_BITS, None,
                                      ALU.logical_shift_right).then_inc(s["meta_chain"], 1)
                    dve.tensor_scalar(col_i[:, bass.ds(par * P, P)], rc_i[:, :], (1 << COL_BITS) - 1, None,
                                      ALU.bitwise_and).then_inc(s["meta"], 1)
                    dve.wait_ge(s["meta_chain"], number * 3 - 1)
                    dve.tensor_copy(rlo_f[:, bass.ds(par * P, P)], rlo_i[:, :]).then_inc(s["meta_chain"], 1)
                    dve.wait_ge(s["meta_chain"], number * 3)
                    dve.sem_inc(s_pass["dve"], 1)

                used = dve.value_load(turns_i[0:1, n:n + 1], min_val=1, max_val=L.blocks)
                take_apart(1, 0)
                with dve.Fori(0, used) as blk:
                    take_apart(blk + 2, (blk + 1) & 1)
                    with dve.Fori(0, TURNS) as i:
                        t = blk * TURNS + i
                        for h in range(2):
                            dve.wait_ge(s["summed"], t * 2 + h + 1)
                            dve.sem_inc(s_pass["dve"], 1)
                            for k in range(h * HALF, (h + 1) * HALF):
                                last = dve.tensor_scalar(spread[:, k, :], iota_f[:, 0:P],
                                                         rlo_f[:, bass.ds((blk & 1) * P + i * NG + k, 1)],
                                                         val_f[:, bass.ds((blk & 1) * P + i * NG + k, 1)], ALU.is_equal, ALU.mult)
                            last.then_inc(s["spread"], 1)
                        for h in range(2):
                            dve.wait_ge(s["summed"], t * 2 + h + 3)
                            dve.sem_inc(s_pass["dve"], 1)
                            for r in range(HR):
                                run = (t * 2 + h) * HR + r
                                b = dve.value_load(binrow[0:1, bass.ds(run, 1)], min_val=0, max_val=L.bins)
                                dst = sums[:, bass.ds(b * D, D)]
                                dve.wait_ge(s["added"], run + (HR + 1))
                                dve.tensor_tensor(dst, dst, sum_ps[h][:, r * D:(r + 1) * D],
                                                  ALU.add).then_inc(s["added"], 1)
                dve.wait_ge(s["added"], used * (P // RUN) + (HR + 1))
                dve.sem_inc(s["done"], 1)
                if n == 0:
                    dve.wait_ge(S[0]["sums_out"], 32)
            for t in range(1, IT, 2):
                dve.wait_ge(s_fin["turned"], t + 1)
                dve.tensor_copy(item_t[:, :, t], fin_ps[t % 2][:, 0:IP]).then_inc(s_fin["turned_dve"], 1)
            for c in range(NBC):
                dve.wait_ge(s_fin["turned"], IT + 4 * (c + 1))
                dve.tensor_copy(batch_t[:, c * 512:(c + 1) * 512], out_ps[c][:, :]).then_inc(s_fin["turned_dve"], 1)
            for t in range(BT):
                if t >= 2:
                    dve.wait_ge(s_fin[("out0", "out1")[t % 2]], 16 * (t // 2))
                for c in range(1, NC, 2):
                    i = t * NC + c
                    wd = min(512, N_SCORE - c * 512)
                    dve.wait_ge(s_fin["o"], i + 1)
                    dve.tensor_copy(orow[t % 2][:, c * 512:c * 512 + wd], out_ps[i % 4][:, 0:wd]).then_inc(s_fin["o_read_dve"], 1)


_INS = ["r_batch_idxes", "L0_rec_emb_table", "L0_rec_W", "L0_rec_b", "L0_rec_sess_vals", "L0_rec_A_vals",
        "L0_rec_item_idxes", "L0_rec_item_emb_idxes", "L0_rec_sess_rows", "L0_rec_sess_cols",
        "L0_rec_A_rows", "L0_rec_A_cols"]


def kernel(**inputs):
    import numpy as _np
    import concourse.bacc as _bacc
    from concourse import mybir as _mybir
    from concourse.bass_utils import run_bass_kernel_spmd as _run

    nc = _bacc.Bacc("TRN2", target_bir_lowering=False, num_devices=1)
    arrays, args = {}, []
    for name in _INS:
        a = _np.ascontiguousarray(inputs[name])
        arrays[f"in_{name}_dram"] = a
        args.append(nc.dram_tensor(f"in_{name}_dram", a.shape, _mybir.dt.from_np(a.dtype), kind="ExternalInput").ap())
    out = nc.dram_tensor("out_dram", (BATCH, N_SCORE), F32, kind="ExternalOutput").ap()
    build_program(nc, *args, out)
    r = _run(nc, [arrays], core_ids=[0])
    return r.results[0]["out_dram"]
```
